# Optimizing a Trainium2 kernel written in Bass

```python
import numpy as np
import jax
import jax.numpy as jnp

def _softmax(x, axis=-1):
    return jax.nn.softmax(x, axis=axis)

def _gelu(x):
    return jax.nn.gelu(x, approximate=True)

def _silu(x):
    return jax.nn.silu(x)

def _sigmoid(x):
    return jax.nn.sigmoid(x)

def _layernorm(x, axis=-1, eps=1e-05):
    m = jnp.mean(x, axis=axis, keepdims=True)
    v = jnp.var(x, axis=axis, keepdims=True)
    return (x - m) / jnp.sqrt(v + eps)

def _scatter_add(tgt, idx, src, axis=0):
    return tgt.at[idx].add(src)

def _segment_sum(src, seg, n):
    return jax.ops.segment_sum(src, seg, n)
kernel_name = 'mk_early_fusion_d1_tok_img1024_r4_b2ac00'

def setup_inputs(seed: int=0):
    np.random.seed(seed)
    _w = jnp.asarray

    def _rec_inputs():
        import jax
        import jax.numpy as jnp
        _rk = jax.random.key(seed)
        x = -0.00150118 + 0.499729 * jax.random.normal(jax.random.fold_in(_rk, 1), (8, 256, 64, 2), jnp.float32)
        txt = 0.00326275 + 2.8086 * jax.random.normal(jax.random.fold_in(_rk, 2), (8, 128, 256), jnp.float32)
        return (x, txt)
    x, txt = _rec_inputs()

    def _L0_tok_setup():
        import jax, jax.numpy as jnp
        import numpy as np
        import math
        H = 256
        N = 64
        CH = 1
        SEQ_L = 256
        key = jax.random.key(seed)
        k1, k2, k3, k4 = jax.random.split(key, 4)
        log_dt = jax.random.uniform(k1, (H,), dtype=jnp.float32, minval=math.log(0.001), maxval=math.log(0.1))
        inv_A_real = jnp.log(0.5 * jnp.ones((H, N), jnp.float32)) + 0.1 * jax.random.normal(k2, (H, N), dtype=jnp.float32)
        A_imag = jnp.broadcast_to(math.pi * jnp.arange(N, dtype=jnp.float32), (H, N)).copy()
        B_ri = jax.random.normal(k3, (H, N, 2), dtype=jnp.float32) * 0.5
        C_ri = jax.random.normal(k4, (CH, H, N, 2), dtype=jnp.float32) * 0.5
        return {'log_dt': log_dt, 'inv_A_real': inv_A_real, 'A_imag': A_imag, 'B_ri': B_ri, 'C_ri': C_ri, 'L': SEQ_L}
    _L0_tok_all = _L0_tok_setup()
    _L0_tok_in = {k: v for k, v in _L0_tok_all.items() if k in ('log_dt', 'inv_A_real', 'A_imag', 'B_ri')}
    del _L0_tok_all

    def _L0_attn_setup():
        import jax, jax.numpy as jnp
        import numpy as np
        T, B, D = (512, 8, 256)
        N_STATE, BLK = (256, 8)
        NB = N_STATE // BLK

        def _reference_tuple_inner(x, W_k, W_v, W_q):
            Tn, Bn, Dn = x.shape
            xf = x.reshape(Tn * Bn, Dn)
            k = (xf @ W_k.T).reshape(Tn, Bn, NB, BLK)
            v = (xf @ W_v.T).reshape(Tn, Bn, NB, BLK)
            q = (xf @ W_q.T).reshape(Tn, Bn, NB, BLK)
            S0 = jnp.zeros((Bn, NB, BLK, BLK), dtype=x.dtype)

            def step(S, kvq):
                k_t, v_t, q_t = kvq
                k_norm = k_t / (jnp.linalg.norm(k_t, axis=-1, keepdims=True) + 1e-06)
                retrieved = jnp.einsum('bnij,bnj->bni', S, k_norm)
                delta = v_t - retrieved
                S_new = jnp.tanh(S + jnp.einsum('bni,bnj->bnij', delta, k_norm))
                Sq = jnp.einsum('bnij,bnj->bni', S_new, q_t).reshape(Bn, NB * BLK)
                out = Sq * jax.nn.silu(Sq)
                return (S_new, out)
            S_final, outputs = jax.lax.scan(step, S0, (k, v, q))
            return (outputs, S_final)
        key = jax.random.key(seed)
        k1, k2, k3, k4 = jax.random.split(key, 4)
        scale = float(np.sqrt(2.0 / (N_STATE + D)))
        return {'x': jax.random.normal(k1, (T, B, D), dtype=jnp.float32), 'W_k': jax.random.normal(k2, (N_STATE, D), dtype=jnp.float32) * scale, 'W_v': jax.random.normal(k3, (N_STATE, D), dtype=jnp.float32) * scale, 'W_q': jax.random.normal(k4, (N_STATE, D), dtype=jnp.float32) * scale}
    _L0_attn_all = _L0_attn_setup()
    _L0_attn_in = {k: v for k, v in _L0_attn_all.items() if k in ('W_k', 'W_v', 'W_q')}
    del _L0_attn_all

    def _L0_ffn_setup():
        import jax, jax.numpy as jnp
        import numpy as np
        D, H, E, K, S = (256, 512, 8, 2, 1)
        B, L = (4, 512)
        key = jax.random.key(seed)
        ks = jax.random.split(key, 9)
        std = 0.02
        return {'x': jax.random.normal(ks[0], (B, L, D), dtype=jnp.float32), 'router_w': jax.random.normal(ks[1], (E, D), dtype=jnp.float32) * std, 'experts_bias': jnp.zeros((E,), dtype=jnp.float32), 'w1': jax.random.normal(ks[2], (E, D, H), dtype=jnp.float32) * std, 'w3': jax.random.normal(ks[3], (E, D, H), dtype=jnp.float32) * std, 'w2': jax.random.normal(ks[4], (E, H, D), dtype=jnp.float32) * std, 'sw1': jax.random.normal(ks[5], (S, D, H), dtype=jnp.float32) * std, 'sw3': jax.random.normal(ks[6], (S, D, H), dtype=jnp.float32) * std, 'sw2': jax.random.normal(ks[7], (S, H, D), dtype=jnp.float32) * std}
    _L0_ffn_all = _L0_ffn_setup()
    _L0_ffn_in = {k: v for k, v in _L0_ffn_all.items() if k in ('router_w', 'experts_bias', 'w1', 'w3', 'w2', 'sw1', 'sw3', 'sw2')}
    del _L0_ffn_all
    return {'x': x, 'txt': txt, 'L0_tok_log_dt': _L0_tok_in['log_dt'], 'L0_tok_inv_A_real': _L0_tok_in['inv_A_real'], 'L0_tok_A_imag': _L0_tok_in['A_imag'], 'L0_tok_B_ri': _L0_tok_in['B_ri'], 'L0_attn_W_k': _L0_attn_in['W_k'], 'L0_attn_W_v': _L0_attn_in['W_v'], 'L0_attn_W_q': _L0_attn_in['W_q'], 'L0_ffn_router_w': _L0_ffn_in['router_w'], 'L0_ffn_experts_bias': _L0_ffn_in['experts_bias'], 'L0_ffn_w1': _L0_ffn_in['w1'], 'L0_ffn_w3': _L0_ffn_in['w3'], 'L0_ffn_w2': _L0_ffn_in['w2'], 'L0_ffn_sw1': _L0_ffn_in['sw1'], 'L0_ffn_sw3': _L0_ffn_in['sw3'], 'L0_ffn_sw2': _L0_ffn_in['sw2']}

def reference(x, txt, L0_tok_log_dt, L0_tok_inv_A_real, L0_tok_A_imag, L0_tok_B_ri, L0_attn_W_k, L0_attn_W_v, L0_attn_W_q, L0_ffn_router_w, L0_ffn_experts_bias, L0_ffn_w1, L0_ffn_w3, L0_ffn_w2, L0_ffn_sw1, L0_ffn_sw3, L0_ffn_sw2):
    import jax
    import jax.numpy as jnp

    def _L0_tok_ref(log_dt, inv_A_real, A_imag, B_ri, C_ri, L):
        import jax, jax.numpy as jnp
        import numpy as np
        import math
        H = 256
        N = 64
        CH = 1
        SEQ_L = 256
        dt = jnp.exp(log_dt)
        A = -jnp.exp(inv_A_real) + 1j * A_imag
        B = B_ri[..., 0] + 1j * B_ri[..., 1]
        C = C_ri[..., 0] + 1j * C_ri[..., 1]
        dtA = A * dt[:, None]
        dA = (1.0 + dtA / 2) / (1.0 - dtA / 2)
        C_term = C * B[None]
        log_dA = jnp.log(dA)
        V = jnp.exp(log_dA[:, :, None] * jnp.arange(L))
        K = 2.0 * jnp.einsum('chn,hnl->chl', C_term, V).real
        return K.astype(jnp.float32)

    def _L0_attn_ref(x, W_k, W_v, W_q):
        import jax, jax.numpy as jnp
        import numpy as np
        T, B, D = (512, 8, 256)
        N_STATE, BLK = (256, 8)
        NB = N_STATE // BLK

        def _reference_tuple_inner(x, W_k, W_v, W_q):
            Tn, Bn, Dn = x.shape
            xf = x.reshape(Tn * Bn, Dn)
            k = (xf @ W_k.T).reshape(Tn, Bn, NB, BLK)
            v = (xf @ W_v.T).reshape(Tn, Bn, NB, BLK)
            q = (xf @ W_q.T).reshape(Tn, Bn, NB, BLK)
            S0 = jnp.zeros((Bn, NB, BLK, BLK), dtype=x.dtype)

            def step(S, kvq):
                k_t, v_t, q_t = kvq
                k_norm = k_t / (jnp.linalg.norm(k_t, axis=-1, keepdims=True) + 1e-06)
                retrieved = jnp.einsum('bnij,bnj->bni', S, k_norm)
                delta = v_t - retrieved
                S_new = jnp.tanh(S + jnp.einsum('bni,bnj->bnij', delta, k_norm))
                Sq = jnp.einsum('bnij,bnj->bni', S_new, q_t).reshape(Bn, NB * BLK)
                out = Sq * jax.nn.silu(Sq)
                return (S_new, out)
            S_final, outputs = jax.lax.scan(step, S0, (k, v, q))
            return (outputs, S_final)
        return _reference_tuple_inner(x, W_k, W_v, W_q)[0]

    def _L0_ffn_ref(x, router_w, experts_bias, w1, w3, w2, sw1, sw3, sw2):
        import jax, jax.numpy as jnp
        import numpy as np
        D, H, E, K, S = (256, 512, 8, 2, 1)
        B, L = (4, 512)
        b, l, d = x.shape
        xf = x.reshape(-1, d)
        sg = jnp.einsum('td,sdh->tsh', xf, sw1)
        su = jnp.einsum('td,sdh->tsh', xf, sw3)
        shared_out = jnp.einsum('tsh,shd->td', jax.nn.silu(sg) * su, sw2)
        logits = xf @ router_w.T + experts_bias
        rw, sel = jax.lax.top_k(logits, K)
        rw = jax.nn.softmax(rw.astype(jnp.float32), axis=-1).astype(x.dtype)
        cw = (jax.nn.one_hot(sel, E, dtype=x.dtype) * rw[..., None]).sum(axis=1)
        g = jnp.einsum('td,edh->teh', xf, w1)
        u = jnp.einsum('td,edh->teh', xf, w3)
        eo = jax.nn.silu(g) * u
        moe_out = jnp.einsum('te,teh,ehd->td', cw, eo, w2)
        return (moe_out + shared_out).reshape(b, l, d)
    h = _L0_tok_ref(L0_tok_log_dt, L0_tok_inv_A_real, L0_tok_A_imag, L0_tok_B_ri, x, 256)
    h = jnp.concatenate([h, txt], axis=1)
    h = h + _L0_attn_ref(_layernorm(h, axis=-1), L0_attn_W_k, L0_attn_W_v, L0_attn_W_q)
    h = h + _L0_ffn_ref(_layernorm(h, axis=-1), L0_ffn_router_w, L0_ffn_experts_bias, L0_ffn_w1, L0_ffn_w3, L0_ffn_w2, L0_ffn_sw1, L0_ffn_sw3, L0_ffn_sw2)
    return h

_drawn_inputs = setup_inputs


def setup_inputs(seed=0):
    import zlib

    import numpy as np

    out = dict(_drawn_inputs(seed))
    spreads = {'L0_ffn_experts_bias': (0.0, 0.8)}
    factors = {'L0_ffn_router_w': 8.0,
     'L0_ffn_w1': 8.0,
     'L0_ffn_w3': 8.0,
     'L0_ffn_w2': 8.0,
     'L0_ffn_sw1': 8.0,
     'L0_ffn_sw3': 8.0,
     'L0_ffn_sw2': 8.0}
    for name, (base, spread) in spreads.items():
        noise = np.random.default_rng([zlib.crc32(name.encode()), seed]).standard_normal(out[name].shape)
        drawn = base * np.exp(spread * noise) if base else spread * noise
        out[name] = jnp.asarray(drawn.astype(out[name].dtype))
    for name, factor in factors.items():
        out[name] = (out[name] * factor).astype(out[name].dtype)
    return out
```

```python
from contextlib import ExitStack

import concourse.bass as bass
from concourse import mybir
from concourse.alu_op_type import AluOpType as ALU

F32 = mybir.dt.float32
U32 = mybir.dt.uint32
ACT = mybir.ActivationFunctionType
AX_X = mybir.AxisListType.X

STAGE = 3

P = 128
LN_EPS = 1e-5
NORM_EPS = 1e-6


def early_fusion_kernel(nc, x, txt, log_dt, inv_A_real, A_imag, B_ri, W_k, W_v, W_q,
                        router_w, experts_bias, w1, w3, w2, sw1, sw3, sw2, out):
    T, H, N, _ = x.shape
    TXT = txt.shape[1]
    D = txt.shape[2]
    HH = H // P
    BT = (H + TXT) // P
    G = T * BT
    BLK = 8
    NB = D // BLK
    E, HID = router_w.shape[0], w1.shape[2]
    KF = D // P
    KH = HID // P
    BQ = 32
    AP_ = D // BQ
    CA = T * AP_
    CH = 16
    NCH = P // CH

    with ExitStack() as ctx:
        def sb(name, shape, dt=F32, c=ctx):
            return c.enter_context(nc.sbuf_tensor(name, shape, dt))

        def ps(name, shape, c=ctx):
            return c.enter_context(nc.psum_tensor(name, shape, F32))

        def sem(name):
            return ctx.enter_context(nc.semaphore(name))

        X = sb("X", [P, G, D])
        ident = sb("ident", [P, P])
        wT = sb("wT", [P, KF, 3 * D])
        rwT = sb("rwT", [P, KF, E])
        biasb = sb("biasb", [P, E])
        mv1 = sb("mv1", [P, G, 2])
        rstd1 = sb("rstd1", [P, G])
        st1 = sb("st1", [P, G, 6])
        sW13 = sb("sW13", [P, 2, KF, HID])
        sW2 = sb("sW2", [P, KH, D])
        logits = sb("logits", [P, G, E])

        ssm = ExitStack()
        inA = sb("inA", [P, HH, N], c=ssm)
        inI = sb("inI", [P, HH, N], c=ssm)
        inB = sb("inB", [P, HH, N, 2], c=ssm)
        inC = sb("inC", [P, T, HH, N, 2], c=ssm)
        wraw = sb("wraw", [P, 3, KF, D], c=ssm)
        rraw = sb("rraw", [E, D], c=ssm)
        dt = sb("dt", [P, P], c=ssm)
        ea = sb("ea", [P, P], c=ssm)
        z = sb("z", [P, 2, P], c=ssm)
        zz = sb("zz", [P, 3, P], c=ssm)
        den = sb("den", [P, 4, P], c=ssm)
        B2 = sb("B2", [P, 4, P], c=ssm)
        Dc = sb("Dc", [P, 2, P, T], c=ssm)
        Dt = sb("Dt", [P, 2, P, T], c=ssm)
        Q = sb("Q", [P, 2, P, BQ + 1], c=ssm)
        Pw = sb("Pw", [P, 2, P, AP_], c=ssm)
        qt = sb("qt", [P, 4, P, BQ // 2], c=ssm)
        Wc = sb("Wc", [P, 2, 2, CH, CA], c=ssm)
        Wt = qt[:].rearrange("p i h w -> p (i h w)").rearrange("p (u i h w) -> p u i h w", u=2, i=4, h=CH)
        Z = sb("Z", [P, BQ, P], c=ssm)
        ssm.close()

        scan = ExitStack()
        KVQ = sb("KVQ", [P, G, 3, D], c=scan)
        S = sb("S", [P, BT, NB, BLK, BLK], c=scan)
        tmp = sb("tmp", [P, BT, NB, BLK, BLK], c=scan)
        tq = sb("tq", [P, NB, BLK, BLK], c=scan)
        xn1 = sb("xn1", [P, BT, D], c=scan)
        xT1 = sb("xT1", [P, KF, P], c=scan)
        ksq = sb("ksq", [P, NB, BLK], c=scan)
        NN = BT * NB
        nv = sb("nv", [P, NN + BT], c=scan)
        sd = sb("sd", [P, NN + BT], c=scan)
        rn = sb("rn", [P, NN + BT], c=scan)
        dl = sb("dl", [P, D], c=scan)
        Sq = sb("Sq", [P, BT, D], c=scan)
        sl = sb("sl", [P, BT, D], c=scan)
        st2 = sb("st2", [P, 6], c=scan)
        xs = sb("xs", [P, BT, D], c=scan)
        ag = sb("ag", [P, 2], c=scan)
        mean2 = sb("mean2", [P, BT], c=scan)
        xn2 = sb("xn2", [P, BT, D], c=scan)
        xT2 = sb("xT2", [P, KF, P], c=scan)
        sg = sb("sg", [P, HID], c=scan)
        aa = sb("aa", [P, HID], c=scan)
        aT = sb("aT", [P, KH, P], c=scan)
        scan.close()

        EW = 3 * KF * HID
        WE = sb("WE", [P, E * EW])
        rk = sb("rk", [P, G, E])
        wt = sb("wt", [P, 2, G])
        top = sb("top", [P, 2, G])
        M = sb("M", [P, 2, G, E])
        va = sb("va", [P, G, E])
        rb = sb("rb", [P, G])
        cw = sb("cw", [P, G, E])
        xg = sb("xg", [P, 2, D])
        xTe = sb("xTe", [P, 2, KF, P])
        sge = sb("sge", [P, 2, HID])
        ae = sb("ae", [P, 2, HID])
        aTe = sb("aTe", [P, 2, KH, P])
        xn2_rows = nc.dram_tensor("xn2_rows", (G * P, D), F32).ap()

        pssm = ExitStack()
        pA = ps("pA", [P, 4, P], pssm)
        pC = ps("pC", [P, 4, 4, P], pssm)
        pW = ps("pW", [P, 3, 512], pssm)
        pssm.close()
        p2 = ExitStack()
        pZ = ps("pZ", [P, 2, CH, BQ], p2)
        pX = ps("pX", [P, 2, 4, HH, T, AP_], p2)
        p2.close()
        tp = ps("tp", [P, 2, D])
        pR = ps("pR", [P, 512])
        pkv = ps("pkv", [P, 2 * D])
        pq = ps("pq", [P, 512])
        pg = ps("pg", [P, HID])
        pu = ps("pu", [P, HID])
        pa = ps("pa", [P, KH, P])
        py = ps("py", [P, 512])

        names = """ld_a ld_c0 ld_c1 ld_b ld_w ld_r ld_txt ld_sh ld_dt ld_bias id0 ident_ready consts
            ta_done tc_done tw_done tr_done exp_done b2_done wt_copied rwt_copied dve_ssm pool_ssm dc_ready
            q_pool_in q_dve w_in wr_ready wi_ready ssm_sum z_copied zt_done xa_copied xd_copied st1_done var1 sd1 rstd1_done s_zero
            xn1_ready t1_done xt1_ready proj_done kvq_ready ksq_ready n2_ready root_ready eps_added rn_ready kn_ready xs_copied nv_one var2_ready mean2_ready
            a1_done a2_done a3_done outer_ready u_ready tanh_done o_ready sq_ready sl_ready h1_ready x2_ready
            st2_done mv2_ready xn2_ready t2_done xt2_ready gu_done sg_ready m_done a_ready
            at_done at_ready y_done y_added logit_ready stored
            xn2_st0 xn2_st1 xn2_st2 ld_we rk_ready route exp2_done w_ready cw_ready xg_ld0 xg_ld1 te_done xte_ready g_done sge_ready
            u_done ae_ready ate_done ate_ready ye_done x_added""".split()
        s = {n: sem(n) for n in names}

        block = ctx.enter_context(nc.Block())

        xv = X[:, :, :].rearrange("p (c q) (a b) -> p c q a b", q=BT, b=BQ)

        AHEAD, LAST_LAG = 2 * BT, 8

        def run_experts(eng, step):
            for e in range(E):
                step(e, 0, e)
            with eng.Fori(1, G - 1) as i:
                for e in range(E):
                    step(i * E + e, i, e)
            for e in range(E):
                step((G - 1) * E + e, G - 1, e)
            step(G * E, G, 0)

        def run(eng, step):
            lo, hi = 3 * BT, G - 2 * BT
            for g in range(lo):
                step(g, lambda lag, g=g: 0 <= g - lag < G)
            with eng.Fori(lo // BT, hi // BT) as t:
                for bt in range(BT):
                    step(t * BT + bt, lambda lag: True, bt, t)
            for g in range(hi, G + LAST_LAG):
                step(g, lambda lag, g=g: 0 <= g - lag < G)

        @block.sync
        def _(sp):
            sp.dma_start(inA[:], inv_A_real.rearrange("(q p) n -> p q n", p=P)).then_inc(s["ld_a"], 16)
            sp.dma_start(inI[:], A_imag.rearrange("(q p) n -> p q n", p=P)).then_inc(s["ld_a"], 16)
            for q in range(HH):
                sp.dma_start(dt[q * N:(q + 1) * N, :],
                             log_dt[q * P:(q + 1) * P].rearrange("(a h) -> a h", a=1).to_broadcast([N, P])
                             ).then_inc(s["ld_dt"], 16)
            for c in range(T):
                sp.dma_start(inC[:, c], x[c].rearrange("(q p) n r -> p q n r", p=P)
                             ).then_inc(s["ld_c0" if c < T // 2 else "ld_c1"], 16)
            sp.dma_start(xv_txt(X, BT), txt.rearrange("t p d -> p t d")).then_inc(s["ld_txt"], 16)
            sp.dma_start(sW13[:, 0], sw1[0].rearrange("(k p) n -> p k n", p=P)).then_inc(s["ld_sh"], 16)
            sp.dma_start(sW13[:, 1], sw3[0].rearrange("(k p) n -> p k n", p=P)).then_inc(s["ld_sh"], 16)
            sp.dma_start(sW2[:], sw2[0].rearrange("(k p) n -> p k n", p=P)).then_inc(s["ld_sh"], 16)

            def load_expert(e):
                for k, w in enumerate((w1, w3, w2)):
                    sp.dma_start(WE[:, e * EW + k * KF * HID:e * EW + (k + 1) * KF * HID].rearrange(
                        "p (k n) -> p k n", n=w.shape[2]), w[e].rearrange("(k p) n -> p k n", p=P)
                        ).then_inc(s["ld_we"], 16)

            def step(g, has, bt=None, t=None):
                b = g % BT if bt is None else bt
                if has(5):
                    i = g - 5
                    sp.wait_ge(s["xn2_ready"], i + 1)
                    rows = xn2_rows.rearrange("(g p) d -> p g d", p=P)[:, ix(i), :]
                    sp.dma_start(rows, xn2[:, (b - 5) % BT][:, None, :]).then_inc(s[f"xn2_st{(b - 5) % BT}"], 16)
                if t is None and g >= G - 2 * BT:
                    for e in range(E):
                        ready = min(4 * e + 4, G)
                        if max(ready, G - 2 * BT) == g:
                            sp.wait_ge(s["o_ready"], ready)
                            load_expert(e)

            run(sp, step)
            for i in range(BT):
                sp.wait_ge(s[f"xn2_st{i}"], 16 * (G // BT))
            rows = xn2_rows.rearrange("(g p) d -> p g d", p=P)
            sp.dma_start(xg[:, 0], rows[:, 0, :]).then_inc(s["xg_ld0"], 16)
            with sp.Fori(1, G) as i:
                sp.wait_ge(s["te_done"], i)
                sp.dma_start(xg[:, 0:1], rows[:, ix(i), :]).then_inc(s["xg_ld0"], 16)
            sp.wait_ge(s["x_added"], E * G)
            ov = out.rearrange("t (q p) d -> p (t q) d", p=P)
            sp.dma_start(ov, X[:]).then_inc(s["stored"], 16)
            sp.wait_ge(s["stored"], 16)

        @block.gpsimd
        def _(pool):
            pool.memset(ident[:], 0.0).then_inc(s["id0"], 1)
            pool.wait_ge(s["id0"], 1)
            pool.affine_select(out=ident[:], in_=ident[:], compare_op=ALU.not_equal, fill=1.0, base=0,
                               pattern=[[-1, P]], channel_multiplier=1).then_inc(s["ident_ready"], 1)
            n = 0
            for k, (A, top) in enumerate(doublings(Q, Pw, BQ, AP_)):
                m, w = top
                pool.wait_ge(s["q_pool_in"], k + 1)
                o = qt[:, 3, :, 0:w]
                pool.tensor_tensor(o, A[:, 1, :, 1:1 + w], A[:, 0, :, m:m + 1].to_broadcast([P, P, w]),
                                   ALU.mult).then_inc(s["pool_ssm"], 1)
                n += 1
                pool.wait_ge(s["pool_ssm"], n)
                pool.wait_ge(s["q_dve"], k + 1)
                pool.tensor_tensor(A[:, 1, :, m + 1:m + 1 + w], qt[:, 2, :, 0:w], o, ALU.add
                                   ).then_inc(s["pool_ssm"], 1)
                n += 1
            pool.wait_ge(s["dc_ready"], 2)
            for j in range(NCH):
                sl_ = slice(j * CH, (j + 1) * CH)
                d = Dc[:, 1, sl_, :, None].to_broadcast([P, CH, T, AP_])
                pp = Pw[:, 0, sl_, None, :].to_broadcast([P, CH, T, AP_])
                w4 = Wt[:, j % 2, 3].rearrange("p h (c a) -> p h c a", a=AP_)
                if j == 0:
                    pool.wait_ge(s["pool_ssm"], n)
                    pool.wait_ge(s["q_pool_in"], n // 2 + 1)
                pool.tensor_tensor(w4, d, pp, ALU.mult).then_inc(s["pool_ssm"], 1)
                n += 1
                pool.wait_ge(s["pool_ssm"], n)
                pool.wait_ge(s["w_in"], j + 1)
                if j >= 2:
                    pool.wait_ge(s["ssm_sum"], j - 1)
                pool.tensor_tensor(Wc[:, j % 2, 1], Wt[:, j % 2, 2], Wt[:, j % 2, 3], ALU.add
                                   ).then_inc(s["wi_ready"], 1)

            def step(g, has, bt=None, t=None):
                b = g % BT if bt is None else bt
                if has(1):
                    c = (b - 1) % BT
                    pool.wait_ge(s["sl_ready"], g)
                    pool.tensor_tensor(sl[:, c], sl[:, c], Sq[:, c], ALU.mult).then_inc(s["h1_ready"], 1)
                if has(0):
                    pool.wait_ge(s["tanh_done"], g + 1)
                    if gt(g, 0):
                        pool.wait_ge(s["sq_ready"], g)
                    q = KVQ[:, ix(g), 2].rearrange("p a (n j) -> p (a n) j", j=BLK)
                    pool.tensor_tensor(tq[:], S[:, b], q[:, :, None, :].to_broadcast([P, NB, BLK, BLK]),
                                       ALU.mult).then_inc(s["o_ready"], 1)
                if has(-2):
                    kn(g + 2, (b + 2) % BT, (g + 2) // BT if t is None else t + (1 if b else 0))

            def kn(i, b, ti):
                if b == 0:
                    pool.wait_ge(s["rn_ready"], ti + 1)
                k = KVQ[:, ix(i), 0].rearrange("p a (n j) -> p (a n) j", j=BLK)
                pool.tensor_tensor(k, k, rn[:, b * NB:(b + 1) * NB, None].to_broadcast([P, NB, BLK]), ALU.mult
                                   ).then_inc(s["kn_ready"], 1)

            kn(0, 0, 0)
            kn(1, 1, 0)
            run(pool, step)

        @block.scalar
        def _(act):
            act.dma_start(inB[:], B_ri.rearrange("(q p) n r -> p q n r", p=P)).then_inc(s["ld_b"], 16)
            for i, w in enumerate((W_k, W_v, W_q)):
                act.dma_start(wraw[:, i], w.rearrange("(k p) f -> p k f", p=P)).then_inc(s["ld_w"], 16)
            act.dma_start(rraw[:], router_w).then_inc(s["ld_r"], 16)
            act.dma_start(biasb[:], experts_bias.rearrange("(a e) -> a e", a=1).to_broadcast([P, E])
                          ).then_inc(s["ld_bias"], 16)
            act.wait_ge(s["ld_dt"], 16 * HH)
            act.activation(dt[:], dt[:], ACT.Exp).then_inc(s["exp_done"], 1)
            act.wait_ge(s["ta_done"], 1)
            act.activation(ea[:], pA[:, 0], ACT.Exp).then_inc(s["exp_done"], 1)
            act.mul(B2[:, 0], pA[:, 2], 2.0).then_inc(s["b2_done"], 1)
            act.mul(B2[:, 1], pA[:, 3], -2.0).then_inc(s["b2_done"], 1)
            act.mul(B2[:, 2], pA[:, 2], -2.0).then_inc(s["b2_done"], 1)
            act.wait_ge(s["tw_done"], 1)
            act.activation(wT[:].rearrange("p k (w o) -> p k w o", w=3), pW[:, :, :].rearrange(
                "p w (k o) -> p k w o", k=KF), ACT.Copy).then_inc(s["wt_copied"], 1)
            act.wait_ge(s["tr_done"], 1)
            act.activation(rwT[:], pA[:, 0, 0:KF * E].rearrange("p (k e) -> p k e", k=KF), ACT.Copy
                           ).then_inc(s["rwt_copied"], 1)
            for j in range(NCH):
                act.wait_ge(s["ssm_sum"], j + 1)
                act.activation(Z[:, :, j * CH:(j + 1) * CH].rearrange("p b h -> p h b"), pZ[:, j % 2], ACT.Copy
                               ).then_inc(s["z_copied"], 1)
            for j in range(BQ // 4):
                act.wait_ge(s["zt_done"], j + 1)
                act.activation(x_slot(xv, 0, j), pX[:, j % 2, :, 0], ACT.Copy).then_inc(s["xa_copied"], 1)
            act.wait_ge(s["var1"], 1)
            act.activation(rstd1[:], rstd1[:], ACT.Sqrt).then_inc(s["sd1"], 1)

            def front(i):
                act.wait_ge(s["t1_done"], i + 1)
                if gt(i, 0):
                    act.wait_ge(s["proj_done"], i)
                act.activation(xT1[:], tp[:, 0].rearrange("p (k n) -> p k n", k=KF), ACT.Copy
                               ).then_inc(s["xt1_ready"], 1)

            def front2(i):
                act.wait_ge(s["proj_done"], i + 1)
                kvq = KVQ[:, ix(i)].rearrange("p a w d -> p (a w) d")
                act.activation(kvq[:, 0:2], pkv[:].rearrange("p (w d) -> p w d", w=2), ACT.Copy
                               ).then_inc(s["kvq_ready"], 1)
                act.activation(kvq[:, 2], pq[:, 0:D], ACT.Copy).then_inc(s["kvq_ready"], 1)
                if gt(i, 0):
                    act.wait_ge(s["n2_ready"], i)
                act.activation(ksq[:].rearrange("p n j -> p (n j)"), pkv[:, 0:D], ACT.Square
                               ).then_inc(s["ksq_ready"], 1)

            def root(n):
                act.wait_ge(s["n2_ready"], min(n * BT + BT, G) if isinstance(n, int) else n * BT + BT)
                if gt(n, 0):
                    act.wait_ge(s["rn_ready"], n)
                act.activation(sd[:], nv[:], ACT.Sqrt).then_inc(s["root_ready"], 1)

            for i in range(AHEAD):
                front(i)
                front2(i)
                if i == BT - 1:
                    act.wait_ge(s["nv_one"], 1)
                    root(0)

            def step(g, has, bt=None, t=None):
                b = g % BT if bt is None else bt
                if b == 1 and any(map(has, (-2, 3, 4, 5))):
                    if has(3):
                        act.wait_ge(s["var2_ready"], g - 2)
                    root((g // BT if t is None else t) + 1)
                if has(7):
                    i = g - 7
                    act.wait_ge(s["gu_done"], i + 1)
                    if gt(i, 0):
                        act.wait_ge(s["m_done"], i)
                    act.activation(sg[:], pg[:], ACT.Silu).then_inc(s["sg_ready"], 1)
                if has(-AHEAD):
                    front(g + AHEAD)
                if has(3):
                    act.wait_ge(s["x2_ready"], g - 2)
                    act.activation(X[:, ix(g - 3)].rearrange("p a d -> p (a d)"), xs[:, (b - 3) % BT], ACT.Copy
                                   ).then_inc(s["xs_copied"], 1)
                if has(-AHEAD):
                    front2(g + AHEAD)
                if has(7):
                    i = g - 7
                    act.wait_ge(s["at_done"], i + 1)
                    if gt(i, 0):
                        act.wait_ge(s["y_done"], i)
                    act.activation(aT[:], pa[:], ACT.Copy).then_inc(s["at_ready"], 1)
                if has(6):
                    i = g - 6
                    act.wait_ge(s["t2_done"], i + 1)
                    if gt(i, 0):
                        act.wait_ge(s["gu_done"], i)
                    act.activation(xT2[:], tp[:, 1].rearrange("p (k n) -> p k n", k=KF), ACT.Copy
                                   ).then_inc(s["xt2_ready"], 1)
                if has(0):
                    act.wait_ge(s["u_ready"], g + 1)
                    act.activation(S[:, b], S[:, b], ACT.Tanh).then_inc(s["tanh_done"], 1)
                if has(1):
                    c = (b - 1) % BT
                    act.wait_ge(s["sq_ready"], g)
                    if gt(g, BT):
                        act.wait_ge(s["x2_ready"], g - BT)
                    act.activation(sl[:, c], Sq[:, c], ACT.Silu).then_inc(s["sl_ready"], 1)

            run(act, step)
            act.wait_ge(s["route"], 12)
            act.activation(wt[:, 0], top[:, 1], ACT.Exp).then_inc(s["exp2_done"], 1)

            act.wait_ge(s["te_done"], 1)
            act.activation(xTe[:, 0], pkv[:, 0:D].rearrange("p (k n) -> p k n", k=KF), ACT.Copy
                           ).then_inc(s["xte_ready"], 1)

            def expert(n, i, e):
                if not (isinstance(i, int) and i == G):
                    act.wait_ge(s["g_done"], n + 1)
                    if gt(n, 1):
                        act.wait_ge(s["ae_ready"], n - 1)
                    act.activation(sge[:, e % 2], pg[:], ACT.Silu).then_inc(s["sge_ready"], 1)
                if gt(n, 0):
                    act.wait_ge(s["ate_done"], n)
                    if gt(n, 2):
                        act.wait_ge(s["ye_done"], n - 2)
                    act.activation(aTe[:, (e - 1) % 2], pa[:], ACT.Copy).then_inc(s["ate_ready"], 1)
                if e == E - 1 and not (isinstance(i, int) and i >= G - 1):
                    act.wait_ge(s["u_done"], n + 1)
                    act.wait_ge(s["te_done"], i + 2)
                    act.activation(xTe[:, 0], pkv[:, 0:D].rearrange("p (k n) -> p k n", k=KF), ACT.Copy
                                   ).then_inc(s["xte_ready"], 1)

            run_experts(act, expert)

        @block.vector
        def _(dve):
            chain = [0]

            def link(ins):
                chain[0] += 1
                ins.then_inc(s["dve_ssm"], 1)
                dve.wait_ge(s["dve_ssm"], chain[0])

            dve.wait_ge(s["exp_done"], 2)
            dve.wait_ge(s["b2_done"], 3)
            link(dve.scalar_tensor_tensor(out=z[:, 0], in0=ea[:], scalar=-0.5, in1=dt[:], op0=ALU.mult, op1=ALU.mult))
            link(dve.scalar_tensor_tensor(out=z[:, 1], in0=pA[:, 1], scalar=0.5, in1=dt[:], op0=ALU.mult, op1=ALU.mult))
            link(dve.tensor_tensor(zz[:, 0:2], z[:], z[:], ALU.mult))
            link(dve.tensor_scalar(den[:, 0], z[:, 0], -1.0, 1.0, ALU.mult, ALU.add))
            link(dve.tensor_tensor(den[:, 1], den[:, 0], den[:, 0], ALU.mult))
            link(dve.tensor_tensor(den[:, 2], den[:, 1], zz[:, 1], ALU.add))
            link(dve.reciprocal(den[:, 3], den[:, 2]))
            link(dve.tensor_tensor(zz[:, 2], zz[:, 0], zz[:, 1], ALU.add))
            link(dve.tensor_scalar(zz[:, 0], zz[:, 2], -1.0, 1.0, ALU.mult, ALU.add))
            dve.memset(Q[:, 0, :, 0:1], 1.0)
            dve.memset(Q[:, 1, :, 0:1], 0.0)
            dve.memset(Pw[:, 0, :, 0:1], 1.0)
            dve.memset(Pw[:, 1, :, 0:1], 0.0)
            dve.tensor_tensor(Q[:, 0, :, 1], zz[:, 0], den[:, 3], ALU.mult).then_inc(s["dve_ssm"], 1)
            chain[0] += 1
            dve.scalar_tensor_tensor(out=Q[:, 1, :, 1], in0=z[:, 1], scalar=2.0, in1=den[:, 3], op0=ALU.mult,
                                     op1=ALU.mult).then_inc(s["q_pool_in"], 1)
            levels = list(doublings(Q, Pw, BQ, AP_))
            for k, (A, (m, w)) in enumerate(levels):
                if k == 0:
                    dve.wait_ge(s["q_pool_in"], 1)
                    dve.wait_ge(s["dve_ssm"], chain[0])
                br, bi = (A[:, r, :, m:m + 1].to_broadcast([P, P, w]) for r in range(2))
                ar, ai = (A[:, r, :, 1:1 + w] for r in range(2))
                if k > 0:
                    dve.wait_ge(s["pool_ssm"], 2 * k)
                    if A is not levels[k - 1][0]:
                        link(dve.tensor_copy(Pw[:, 0, :, 1], Q[:, 0, :, BQ]))
                        dve.tensor_scalar(Pw[:, 1, :, 1], Q[:, 1, :, BQ], -1.0, None, ALU.mult
                                          ).then_inc(s["q_pool_in"], 1)
                        dve.wait_ge(s["q_pool_in"], k + 1)
                dve.tensor_tensor(qt[:, 2, :, 0:w], ar, bi, ALU.mult).then_inc(s["q_dve"], 1)
                link(dve.tensor_tensor(qt[:, 0, :, 0:w], ar, br, ALU.mult))
                link(dve.tensor_tensor(qt[:, 1, :, 0:w], ai, bi, ALU.mult))
                dve.tensor_tensor(A[:, 0, :, m + 1:m + 1 + w], qt[:, 0, :, 0:w], qt[:, 1, :, 0:w], ALU.subtract
                                  ).then_inc(s["dve_ssm"], 1)
                chain[0] += 1
                dve.wait_ge(s["dve_ssm"], chain[0])
                if k + 1 < len(levels) and levels[k + 1][0] is A:
                    dve.wait_ge(s["pool_ssm"], 2 * k + 2)
                    dve.engine_nop().then_inc(s["q_pool_in"], 1)
                if k == 0:
                    pass
            dve.engine_nop().then_inc(s["q_pool_in"], 1)
            dve.wait_ge(s["tc_done"], 1)
            dve.wait_ge(s["b2_done"], 3)
            cr = pC[:].rearrange("p u v h -> p (u v) h").rearrange("p (c r) h -> p r h c", r=2)
            for o, (re, im) in enumerate(((0, 1), (1, 2))):
                d2 = [B2[:, i, :, None].to_broadcast([P, P, T]) for i in (re, im)]
                link(dve.tensor_tensor(Dc[:, o], cr[:, 0], d2[0], ALU.mult))
                link(dve.tensor_tensor(Dt[:, o], cr[:, 1], d2[1], ALU.mult))
                dve.tensor_tensor(Dc[:, o], Dc[:, o], Dt[:, o], ALU.add).then_inc(s["dc_ready"], 1)
            dve.wait_ge(s["dc_ready"], 2)
            dve.wait_ge(s["pool_ssm"], 2 * len(levels))
            nl = 2 * len(levels)
            for j in range(NCH):
                sl_ = slice(j * CH, (j + 1) * CH)
                d = [Dc[:, r, sl_, :, None].to_broadcast([P, CH, T, AP_]) for r in range(2)]
                pp = [Pw[:, r, sl_, None, :].to_broadcast([P, CH, T, AP_]) for r in range(2)]
                w4 = [Wt[:, j % 2, i].rearrange("p h (c a) -> p h c a", a=AP_) for i in range(4)]
                if j >= 2:
                    dve.wait_ge(s["wi_ready"], j - 1)
                dve.tensor_tensor(w4[2], d[0], pp[1], ALU.mult).then_inc(s["w_in"], 1)
                link(dve.tensor_tensor(w4[0], d[0], pp[0], ALU.mult))
                link(dve.tensor_tensor(w4[1], d[1], pp[1], ALU.mult))
                if j >= 2:
                    dve.wait_ge(s["ssm_sum"], j - 1)
                dve.tensor_tensor(Wc[:, j % 2, 0], Wt[:, j % 2, 0], Wt[:, j % 2, 1], ALU.subtract
                                  ).then_inc(s["wr_ready"], 1)
            for j in range(BQ // 4):
                dve.wait_ge(s["xa_copied"], j + 1)
                dve.tensor_copy(x_slot(xv, 1, j), pX[:, j % 2, :, 1]).then_inc(s["xd_copied"], 1)
            dve.wait_ge(s["xd_copied"], BQ // 4)
            dve.wait_ge(s["ld_txt"], 16)
            for g in range(G):
                dve.bn_stats(st1[:, g], X[:, g]).then_inc(s["st1_done"], 1)
            for g in range(G):
                dve.wait_ge(s["st1_done"], g + 1)
                dve.bn_aggr(mv1[:, g], st1[:, g]).then_inc(s["st1_done"], 1)
            dve.wait_ge(s["st1_done"], 2 * G)
            dve.tensor_scalar(rstd1[:], mv1[:, :, 1], LN_EPS, None, ALU.add).then_inc(s["var1"], 1)
            dve.wait_ge(s["sd1"], 1)
            dve.reciprocal(rstd1[:], rstd1[:]).then_inc(s["rstd1_done"], 1)
            dve.memset(S[:], 0.0).then_inc(s["s_zero"], 1)
            dve.wait_ge(s["rstd1_done"], 1)
            dve.wait_ge(s["s_zero"], 1)

            def front(i, b):
                if gt(i, BT - 1):
                    dve.wait_ge(s["t1_done"], i - BT + 1)
                dve.tensor_scalar(xn1[:, b], X[:, ix(i)].rearrange("p a d -> p (a d)"), mv1[:, ix(i), 0:1].rearrange("p a b -> p (a b)"),
                                  rstd1[:, ix(i)], ALU.subtract, ALU.mult).then_inc(s["xn1_ready"], 1)

            def norm(i, b):
                dve.wait_ge(s["ksq_ready"], i + 1)
                dve.tensor_reduce(nv[:, b * NB:(b + 1) * NB], ksq[:], AX_X, ALU.add).then_inc(s["n2_ready"], 1)

            def roots(n):
                dve.wait_ge(s["root_ready"], n + 1)
                dve.tensor_scalar(sd[:, 0:NN], sd[:, 0:NN], NORM_EPS, None, ALU.add).then_inc(s["eps_added"], 1)
                dve.wait_ge(s["eps_added"], n + 1)
                dve.reciprocal(rn[:], sd[:]).then_inc(s["rn_ready"], 1)

            dve.memset(nv[:], 1.0).then_inc(s["nv_one"], 1)
            dve.wait_ge(s["nv_one"], 1)
            dve.wait_ge(s["ld_bias"], 16)
            for i in range(BT):
                front(i, i)
            for i in range(BT):
                norm(i, i)
            for i in range(BT, AHEAD):
                front(i, i % BT)
            roots(0)
            for i in range(BT, AHEAD - 1):
                norm(i, i % BT)

            def read(i, b):
                k = KVQ[:, ix(i), 0].rearrange("p a (n j) -> p (a n) j", j=BLK)
                dve.wait_ge(s["kn_ready"], i + 1)
                if gt(i, BT - 1):
                    dve.wait_ge(s["tanh_done"], i - 2)
                dve.tensor_tensor(tmp[:, b], S[:, b], k[:, :, None, :].to_broadcast([P, NB, BLK, BLK]), ALU.mult
                                  ).then_inc(s["a1_done"], 1)

            read(0, 0)

            def step(g, has, bt=None, t=None):
                b = g % BT if bt is None else bt
                ti = g // BT if t is None else t
                if has(-AHEAD):
                    front(g + AHEAD, b)
                if has(-1):
                    read(g + 1, (b + 1) % BT)
                if has(7):
                    i = g - 7
                    dve.wait_ge(s["sg_ready"], i + 1)
                    if gt(i, 0):
                        dve.wait_ge(s["at_done"], i)
                    dve.tensor_tensor(aa[:], sg[:], pu[:], ALU.mult).then_inc(s["m_done"], 1)
                    dve.tensor_tensor(logits[:, ix(i)].rearrange("p a e -> p (a e)"), py[:, D:D + E], biasb[:],
                                      ALU.add).then_inc(s["logit_ready"], 1)
                if has(8):
                    i = g - 8
                    xr = X[:, ix(i)].rearrange("p a d -> p (a d)")
                    dve.wait_ge(s["y_done"], i + 1)
                    dve.tensor_tensor(xr, xr, py[:, 0:D], ALU.add).then_inc(s["y_added"], 1)
                if has(-5):
                    if b == 1:
                        dve.wait_ge(s["root_ready"], ti + 2)
                    norm(g + 5, (b + 5) % BT)
                if has(0):
                    kvq = KVQ[:, ix(g)].rearrange("p a w d -> p (a w) d")
                    k = kvq[:, 0].rearrange("p (n j) -> p n j", j=BLK)[:, :, None, :].to_broadcast([P, NB, BLK, BLK])
                    dve.wait_ge(s["a2_done"], g + 1)
                    dve.tensor_tensor(dl[:], kvq[:, 1], pR[:, 0:D], ALU.subtract).then_inc(s["a3_done"], 1)
                    dve.wait_ge(s["a3_done"], g + 1)
                    dve.tensor_tensor(tmp[:, b], dl[:].rearrange("p (n i) -> p n i", i=BLK)[:, :, :, None]
                                      .to_broadcast([P, NB, BLK, BLK]), k, ALU.mult).then_inc(s["outer_ready"], 1)
                if b == 1 and any(map(has, (-2, 3, 4, 5))):
                    roots(ti + 1)
                if has(0):
                    dve.wait_ge(s["outer_ready"], g + 1)
                    if gt(g, BT - 1):
                        dve.wait_ge(s["o_ready"], g - 2)
                    dve.tensor_tensor(S[:, b], S[:, b], tmp[:, b], ALU.add).then_inc(s["u_ready"], 1)
                if has(1):
                    c = (b - 1) % BT
                    dve.wait_ge(s["o_ready"], g)
                    if gt(g, BT):
                        dve.wait_ge(s["h1_ready"], g - BT)
                    dve.tensor_reduce(Sq[:, c].rearrange("p (n i) -> p n i", i=BLK), tq[:], AX_X, ALU.add
                                      ).then_inc(s["sq_ready"], 1)
                if has(2):
                    i = g - 2
                    c = (b - 2) % BT
                    xr = X[:, ix(i)].rearrange("p a d -> p (a d)")
                    dve.wait_ge(s["h1_ready"], i + 1)
                    if gt(i, BT - 1):
                        dve.wait_ge(s["xs_copied"], i - BT + 1)
                    dve.tensor_tensor(xs[:, c], xr, sl[:, c], ALU.add).then_inc(s["x2_ready"], 1)
                    dve.wait_ge(s["x2_ready"], i + 1)
                    dve.bn_stats(st2[:], xs[:, c]).then_inc(s["st2_done"], 1)
                    dve.wait_ge(s["st2_done"], i + 1)
                if has(5):
                    i = g - 5
                    c = (b - 5) % BT
                    if b == 1:
                        dve.wait_ge(s["rn_ready"], ti + 2)
                    if gt(i, BT - 1):
                        dve.wait_ge(s["t2_done"], i - BT + 1)
                        dve.wait_ge(s[f"xn2_st{c}"], 16 * (ti - 2 + (1 if b == 2 else 0)))
                    dve.wait_ge(s["xs_copied"], i + 1)
                    dve.tensor_scalar(xn2[:, c], X[:, ix(i)].rearrange("p a d -> p (a d)"), mean2[:, c:c + 1],
                                      rn[:, NN + c:NN + c + 1], ALU.subtract, ALU.mult
                                      ).then_inc(s["xn2_ready"], 1)
                if has(2):
                    c = (b - 2) % BT
                    dve.bn_aggr(ag[:], st2[:]).then_inc(s["mv2_ready"], 1)
                    dve.wait_ge(s["mv2_ready"], g - 1)
                    dve.tensor_copy(mean2[:, c:c + 1], ag[:, 0:1]).then_inc(s["mean2_ready"], 1)
                    dve.tensor_scalar(nv[:, NN + c:NN + c + 1], ag[:, 1:2], LN_EPS, None, ALU.add
                                      ).then_inc(s["var2_ready"], 1)

            run(dve, step)

            dve.wait_ge(s["ld_we"], 16 * 3 * E)
            for e in range(E):
                dve.memset(rk[:, :, e:e + 1], float(E - e)).then_inc(s["rk_ready"], 1)
            dve.wait_ge(s["rk_ready"], E)
            dve.wait_ge(s["logit_ready"], G)
            nr = [0]

            def then(ins):
                nr[0] += 1
                ins.then_inc(s["route"], 1)
                dve.wait_ge(s["route"], nr[0])

            full = [P, G, E]
            src = logits[:]
            for c in range(2):
                then(dve.tensor_reduce(top[:, c], src, AX_X, ALU.max))
                then(dve.tensor_tensor(va[:], src, top[:, c, :, None].to_broadcast(full), ALU.is_equal))
                then(dve.tensor_tensor(va[:], va[:], rk[:], ALU.mult))
                then(dve.tensor_reduce(rb[:], va[:], AX_X, ALU.max))
                then(dve.tensor_tensor(M[:, c], va[:], rb[:, :, None].to_broadcast(full), ALU.is_equal))
                if c == 0:
                    then(dve.scalar_tensor_tensor(out=cw[:], in0=M[:, 0], scalar=-3.0e38, in1=logits[:],
                                                  op0=ALU.mult, op1=ALU.add))
                    src = cw[:]
            then(dve.tensor_tensor(top[:, 1], top[:, 1], top[:, 0], ALU.subtract))
            dve.wait_ge(s["exp2_done"], 1)
            then(dve.tensor_scalar(wt[:, 1], wt[:, 0], 1.0, None, ALU.add))
            then(dve.reciprocal(rb[:], wt[:, 1]))
            then(dve.tensor_tensor(wt[:, 1], wt[:, 0], rb[:], ALU.mult))
            then(dve.tensor_tensor(cw[:], M[:, 0], rb[:, :, None].to_broadcast(full), ALU.mult))
            then(dve.tensor_tensor(va[:], M[:, 1], wt[:, 1, :, None].to_broadcast(full), ALU.mult))
            then(dve.tensor_tensor(cw[:], cw[:], va[:], ALU.add))

            def expert(n, i, e):
                if not (isinstance(i, int) and i == G):
                    dve.wait_ge(s["sge_ready"], n + 1)
                    dve.wait_ge(s["u_done"], n + 1)
                    if gt(n, 1):
                        dve.wait_ge(s["ate_done"], n - 1)
                    dve.tensor_tensor(ae[:, e % 2], sge[:, e % 2], pu[:], ALU.mult).then_inc(s["ae_ready"], 1)
                if gt(n, 0):
                    j = i if e else i - 1
                    c = (e - 1) % E
                    xr = X[:, ix(j)].rearrange("p a d -> p (a d)")
                    dve.wait_ge(s["ye_done"], n)
                    if gt(n, 1):
                        dve.wait_ge(s["x_added"], n - 1)
                    yb = (pR, py)[c % 2]
                    dve.scalar_tensor_tensor(out=xr, in0=yb[:, 0:D], scalar=cw[:, ix(j), c:c + 1].rearrange(
                        "p a b -> p (a b)"), in1=xr, op0=ALU.mult, op1=ALU.add).then_inc(s["x_added"], 1)

            run_experts(dve, expert)

        @block.tensor
        def _(pe):
            pe.wait_ge(s["ident_ready"], 1)
            pe.wait_ge(s["ld_a"], 32)
            pe.wait_ge(s["ld_b"], 16)
            bv = inB[:].rearrange("p q n r -> p r q n")
            for i, src in enumerate((inA[:], inI[:], bv[:, 0], bv[:, 1])):
                mm = pe.transpose(pA[:, i], src, ident[:])
            mm.then_inc(s["ta_done"], 1)
            for c in range(T):
                if c % (T // 2) == 0:
                    pe.wait_ge(s["ld_c0" if c == 0 else "ld_c1"], 16 * (T // 2))
                cv = inC[:, c].rearrange("p q n r -> p r q n")
                for r in range(2):
                    i = 2 * c + r
                    mm = pe.transpose(pC[:, i // 4, i % 4], cv[:, r], ident[:])
            mm.then_inc(s["tc_done"], 1)
            pe.wait_ge(s["ld_w"], 48)
            for w in range(3):
                for k in range(KF):
                    for o in range(KF):
                        mm = pe.transpose(pW[:, w, k * D + o * P:k * D + (o + 1) * P],
                                          wraw[:, w, o, k * P:(k + 1) * P], ident[:])
            mm.then_inc(s["tw_done"], 1)
            pe.wait_ge(s["ld_r"], 16)
            pe.wait_ge(s["q_pool_in"], 1)
            pe.wait_ge(s["b2_done"], 3)
            for k in range(KF):
                mm = pe.transpose(pA[:, 0, k * E:(k + 1) * E], rraw[:, k * P:(k + 1) * P], ident[0:E, 0:E])
            mm.then_inc(s["tr_done"], 1)

            pe.wait_ge(s["wt_copied"], 1)
            pe.wait_ge(s["rwt_copied"], 1)
            pe.wait_ge(s["dc_ready"], 2)
            for j in range(NCH):
                pe.wait_ge(s["wr_ready"], j + 1)
                pe.wait_ge(s["wi_ready"], j + 1)
                if j >= 2:
                    pe.wait_ge(s["z_copied"], j - 1)
                for h in range(CH):
                    for q in range(HH):
                        r0 = q * N
                        for r in range(2):
                            mm = pe.matmul(pZ[r0:r0 + CA, j % 2, h], Wc[r0:r0 + N, j % 2, r, h],
                                           Q[r0:r0 + N, r, j * CH + h, 0:BQ], start=(r == 0), stop=(r == 1))
                mm.then_inc(s["ssm_sum"], 1)
            pe.wait_ge(s["z_copied"], NCH)
            for j in range(BQ // 4):
                if j >= 2:
                    pe.wait_ge(s["xd_copied"], j - 1)
                for b in range(4):
                    mm = pe.transpose(pX[:, j % 2, b], Z[:, 4 * j + b], ident[:])
                mm.then_inc(s["zt_done"], 1)
            pe.wait_ge(s["xd_copied"], BQ // 4)

            def turn1(i, b):
                pe.wait_ge(s["xn1_ready"], i + 1)
                if gt(i, 0):
                    pe.wait_ge(s["xt1_ready"], i)
                for k in range(KF):
                    mm = pe.transpose(tp[:, 0, k * P:(k + 1) * P], xn1[:, b, k * P:(k + 1) * P], ident[:])
                mm.then_inc(s["t1_done"], 1)

            def project(i):
                pe.wait_ge(s["xt1_ready"], i + 1)
                if gt(i, 0):
                    pe.wait_ge(s["kvq_ready"], 2 * i)
                    pe.wait_ge(s["ksq_ready"], i)
                for k in range(KF):
                    pe.matmul(pkv[:], xT1[:, k], wT[:, k, 0:2 * D], start=(k == 0), stop=(k == KF - 1))
                    mm = pe.matmul(pq[:, 0:D], xT1[:, k], wT[:, k, 2 * D:3 * D], start=(k == 0), stop=(k == KF - 1))
                mm.then_inc(s["proj_done"], 1)

            for i in range(AHEAD):
                turn1(i, i % BT)
                project(i)
            pe.wait_ge(s["ld_sh"], 48)

            def read_sum(i, b):
                pe.wait_ge(s["a1_done"], i + 1)
                if gt(i, 0):
                    pe.wait_ge(s["a3_done"], i)
                for jj in range(BLK):
                    mm = pe.matmul(pR[:, 0:D], ident[:], tmp[:, b, :, :, jj], start=(jj == 0), stop=(jj == BLK - 1))
                mm.then_inc(s["a2_done"], 1)

            read_sum(0, 0)

            def step(g, has, bt=None, t=None):
                b = g % BT if bt is None else bt
                if has(-AHEAD):
                    turn1(g + AHEAD, b)
                    project(g + AHEAD)
                if has(7):
                    i = g - 7
                    pe.wait_ge(s["m_done"], i + 1)
                    if gt(i, 0):
                        pe.wait_ge(s["at_ready"], i)
                    for k in range(KH):
                        mm = pe.transpose(pa[:, k], aa[:, k * P:(k + 1) * P], ident[:])
                    mm.then_inc(s["at_done"], 1)
                if has(-1):
                    read_sum(g + 1, (b + 1) % BT)
                if has(6):
                    i = g - 6
                    pe.wait_ge(s["xn2_ready"], i + 1)
                    if gt(i, 0):
                        pe.wait_ge(s["xt2_ready"], i)
                    for k in range(KF):
                        mm = pe.transpose(tp[:, 1, k * P:(k + 1) * P], xn2[:, b, k * P:(k + 1) * P], ident[:])
                    mm.then_inc(s["t2_done"], 1)
                if has(7):
                    i = g - 7
                    pe.wait_ge(s["at_ready"], i + 1)
                    if gt(i, 0):
                        pe.wait_ge(s["y_added"], i)
                        pe.wait_ge(s["logit_ready"], i + 1)
                    for k in range(KH):
                        mm = pe.matmul(py[:, 0:D], aT[:, k], sW2[:, k], start=(k == 0), stop=(k == KH - 1))
                    mm.then_inc(s["y_done"], 1)
                if has(6):
                    i = g - 6
                    pe.wait_ge(s["xt2_ready"], i + 1)
                    if gt(i, 0):
                        pe.wait_ge(s["logit_ready"], i)
                    if has(8):
                        pe.wait_ge(s["y_added"], i - 1)
                    for k in range(KF):
                        pe.matmul(py[:, D:D + E], xT2[:, k], rwT[:, k], start=(k == 0), stop=(k == KF - 1))
                    for w, dst in ((0, pg), (1, pu)):
                        for k in range(KF):
                            mm = pe.matmul(dst[:], xT2[:, k], sW13[:, w, k], start=(k == 0), stop=(k == KF - 1))
                    mm.then_inc(s["gu_done"], 1)

            run(pe, step)
            pe.wait_ge(s["ld_we"], 16 * 3 * E)
            pe.wait_ge(s["logit_ready"], G)

            def turn(i):
                pe.wait_ge(s["xg_ld0"], 16 * (i + 1))
                if gt(i, 0):
                    pe.wait_ge(s["xte_ready"], i)
                for k in range(KF):
                    mm = pe.transpose(pkv[:, k * P:(k + 1) * P], xg[:, 0, k * P:(k + 1) * P], ident[:])
                mm.then_inc(s["te_done"], 1)

            turn(0)

            def expert(n, i, e):
                now = not (isinstance(i, int) and i == G)
                xt = xTe[:, 0]
                if now:
                    pe.wait_ge(s["xte_ready"], i + 1)
                    if gt(n, 0):
                        pe.wait_ge(s["sge_ready"], n)
                    o = e * EW
                    for k in range(KF):
                        mm = pe.matmul(pg[:], xt[:, k], WE[:, o + k * HID:o + (k + 1) * HID],
                                       start=(k == 0), stop=(k == KF - 1))
                    mm.then_inc(s["g_done"], 1)
                if gt(n, 0):
                    pe.wait_ge(s["ae_ready"], n)
                    if gt(n, 1):
                        pe.wait_ge(s["ate_ready"], n - 1)
                    for k in range(KH):
                        mm = pe.transpose(pa[:, k], ae[:, (e - 1) % 2, k * P:(k + 1) * P], ident[:])
                    mm.then_inc(s["ate_done"], 1)
                if now:
                    o = e * EW + KF * HID
                    for k in range(KF):
                        mm = pe.matmul(pu[:], xt[:, k], WE[:, o + k * HID:o + (k + 1) * HID],
                                       start=(k == 0), stop=(k == KF - 1))
                    mm.then_inc(s["u_done"], 1)
                if gt(n, 0):
                    o = e * EW if e else E * EW
                    o -= KH * D
                    pe.wait_ge(s["ate_ready"], n)
                    if gt(n, 2):
                        pe.wait_ge(s["x_added"], n - 2)
                    yb = (pR, py)[(e - 1) % 2]
                    for k in range(KH):
                        mm = pe.matmul(yb[:, 0:D], aTe[:, (e - 1) % 2, k], WE[:, o + k * D:o + (k + 1) * D],
                                       start=(k == 0), stop=(k == KH - 1))
                    mm.then_inc(s["ye_done"], 1)
                if e == E - 1 and not (isinstance(i, int) and i >= G - 1):
                    turn(i + 1)

            run_experts(pe, expert)


def ix(i):
    return bass.ds(i, 1)


def gt(i, n):
    return not isinstance(i, int) or i > n


def doublings(Q, Pw, BQ, AP_):
    m = 1
    while m < BQ:
        yield Q, (m, m)
        m *= 2
    m = 1
    while m < AP_ - 1:
        yield Pw, (m, min(m, AP_ - 1 - m))
        m *= 2


def x_slot(xv, q, j):
    return xv[:, :, q, :, 4 * j:4 * j + 4].rearrange("p c a b -> p b c a")


def xv_txt(X, BT):
    return X[:, :, :].rearrange("p (t q) d -> p t q d", q=BT)[:, :, BT - 1, :]


_INS = ['x', 'txt', 'L0_tok_log_dt', 'L0_tok_inv_A_real', 'L0_tok_A_imag', 'L0_tok_B_ri', 'L0_attn_W_k',
        'L0_attn_W_v', 'L0_attn_W_q', 'L0_ffn_router_w', 'L0_ffn_experts_bias', 'L0_ffn_w1', 'L0_ffn_w3',
        'L0_ffn_w2', 'L0_ffn_sw1', 'L0_ffn_sw3', 'L0_ffn_sw2']
_OUTS = [((8, 384, 256), 'float32')]


def kernel(**inputs):
    import numpy as _np
    import concourse.bacc as _bacc
    from concourse import mybir as _mybir
    from concourse.bass_utils import run_bass_kernel_spmd as _run

    nc = _bacc.Bacc("TRN2", target_bir_lowering=False, num_devices=1)
    arrays, args = {}, []
    for name in _INS:
        a = _np.ascontiguousarray(inputs[name])
        arrays[f"in_{name}_dram"] = a
        args.append(nc.dram_tensor(f"in_{name}_dram", a.shape, _mybir.dt.from_np(a.dtype), kind="ExternalInput").ap())
    for i, (shape, dtype) in enumerate(_OUTS):
        dt = _mybir.dt.from_np(_np.dtype(dtype))
        args.append(nc.dram_tensor(f"out_{i}_dram", shape, dt, kind="ExternalOutput").ap())
    early_fusion_kernel(nc, *args)
    r = _run(nc, [arrays], core_ids=[0])
    return r.results[0]["out_0_dram"]
```

```python
from contextlib import ExitStack

import concourse.bass as bass
from concourse import mybir
from concourse.alu_op_type import AluOpType as ALU

F32 = mybir.dt.float32
I32 = mybir.dt.int32
ACT = mybir.ActivationFunctionType
AX_X = mybir.AxisListType.X

P = 128
LN_EPS = 1e-5
NORM_EPS = 1e-6


def early_fusion_kernel(nc, x, txt, log_dt, inv_A_real, A_imag, B_ri, W_k, W_v, W_q,
                        router_w, experts_bias, w1, w3, w2, sw1, sw3, sw2, out):
    T, H, N, _ = x.shape
    TXT = txt.shape[1]
    D = txt.shape[2]
    HH = H // P
    BT = (H + TXT) // P
    G = T * BT
    BLK = 8
    NB = D // BLK
    E, HID = router_w.shape[0], w1.shape[2]
    KF = D // P
    KH = HID // P
    BQ = 32
    AP_ = D // BQ
    CA = T * AP_
    NS = 2 * G + E - 1
    CG = G // 2
    CH = 16
    NCH = P // CH

    with ExitStack() as ctx:
        def sb(name, shape, dt=F32, c=ctx):
            return c.enter_context(nc.sbuf_tensor(name, shape, dt))

        def ps(name, shape, c=ctx):
            return c.enter_context(nc.psum_tensor(name, shape, F32))

        def sem(name):
            return ctx.enter_context(nc.semaphore(name))

        X = sb("X", [P, G, D])
        ident = sb("ident", [P, P])
        wT = sb("wT", [P, KF, 3 * D])
        rwT = sb("rwT", [P, KF, E])
        biasb = sb("biasb", [P, E])
        mv1 = sb("mv1", [P, G, 2])
        rstd1 = sb("rstd1", [P, G])
        st1 = sb("st1", [P, G, 6])
        sW13 = sb("sW13", [P, 2, KF, HID])
        sW2 = sb("sW2", [P, KH, D])
        logits = sb("logits", [P, G, E])
        tri = sb("tri", [P, P])
        ones = sb("ones", [P, P])
        iota = sb("iota", [P, P])
        row1 = sb("row1", [P, G])
        pad1 = sb("pad1", [P, 1])
        steps = sb("steps", [P, G])
        rk = sb("rk", [P, E])

        ssm = ExitStack()
        inA = sb("inA", [P, HH, N], c=ssm)
        inI = sb("inI", [P, HH, N], c=ssm)
        inB = sb("inB", [P, HH, N, 2], c=ssm)
        inC = sb("inC", [P, T, HH, N, 2], c=ssm)
        wraw = sb("wraw", [P, 3, KF, D], c=ssm)
        rraw = sb("rraw", [E, D], c=ssm)
        dt = sb("dt", [P, P], c=ssm)
        ea = sb("ea", [P, P], c=ssm)
        z = sb("z", [P, 2, P], c=ssm)
        zz = sb("zz", [P, 3, P], c=ssm)
        den = sb("den", [P, 4, P], c=ssm)
        B2 = sb("B2", [P, 4, P], c=ssm)
        Dc = sb("Dc", [P, 2, P, T], c=ssm)
        Dt = sb("Dt", [P, 2, P, T], c=ssm)
        Q = sb("Q", [P, 2, P, BQ + 1], c=ssm)
        Pw = sb("Pw", [P, 2, P, AP_], c=ssm)
        qt = sb("qt", [P, 4, P, BQ // 2], c=ssm)
        Wc = sb("Wc", [P, 2, 2, CH, CA], c=ssm)
        Wt = qt[:].rearrange("p i h w -> p (i h w)").rearrange("p (u i h w) -> p u i h w", u=2, i=4, h=CH)
        Z = sb("Z", [P, BQ, P], c=ssm)
        ssm.close()

        scan = ExitStack()
        KVQ = sb("KVQ", [P, G, 3, D], c=scan)
        S = sb("S", [P, BT, NB, BLK, BLK], c=scan)
        tmp = sb("tmp", [P, BT, NB, BLK, BLK], c=scan)
        tq = sb("tq", [P, NB, BLK, BLK], c=scan)
        xn1 = sb("xn1", [P, BT, D], c=scan)
        xT1 = sb("xT1", [P, KF, P], c=scan)
        ksq = sb("ksq", [P, NB, BLK], c=scan)
        NN = BT * NB
        nv = sb("nv", [P, NN + BT], c=scan)
        sd = sb("sd", [P, NN + BT], c=scan)
        rn = sb("rn", [P, NN + BT], c=scan)
        dl = sb("dl", [P, D], c=scan)
        Sq = sb("Sq", [P, BT, D], c=scan)
        sl = sb("sl", [P, BT, D], c=scan)
        st2 = sb("st2", [P, 6], c=scan)
        xs = sb("xs", [P, BT, D], c=scan)
        ag = sb("ag", [P, 2], c=scan)
        mean2 = sb("mean2", [P, BT], c=scan)
        xn2 = sb("xn2", [P, BT, D], c=scan)
        xT2 = sb("xT2", [P, KF, P], c=scan)
        sg = sb("sg", [P, HID], c=scan)
        aa = sb("aa", [P, HID], c=scan)
        aT = sb("aT", [P, KH, P], c=scan)
        scan.close()

        EW = 3 * KF * HID
        WE = sb("WE", [P, E * EW])
        wslot = sb("wslot", [P, NS])
        gidx = sb("gidx", [P, NS])
        sidx = sb("sidx", [P, NS])
        etab = sb("etab", [1, NS], I32)
        route_mem = ExitStack()
        wt = sb("wt", [P, 2, G], c=route_mem)
        den2 = sb("den2", [P, G], c=route_mem)
        top = sb("top", [P, 2, G], c=route_mem)
        M = sb("M", [P, 2, G, E], c=route_mem)
        Mc = sb("Mc", [P, G, E], c=route_mem)
        va = sb("va", [P, G, E], c=route_mem)
        rb = sb("rb", [P, G], c=route_mem)
        cnt = sb("cnt", [P, 2, G, E], c=route_mem)
        pos = sb("pos", [P, G, E], c=route_mem)
        over = sb("over", [P, E, G], c=route_mem)
        ends = sb("ends", [P, 3, E], c=route_mem)
        sp_ = sb("slot_pos", [P, 2, G, E], c=route_mem)
        slot = sb("slot", [P, 2, G], c=route_mem)
        sloti = sb("sloti", [P, 3, 2, G], I32, c=route_mem)
        slotf = sb("slotf", [P, 2, 2, G], c=route_mem)
        eq = sb("eq", [P, 2, CG, NS], c=route_mem)
        A1 = sb("A1", [P, 2 * G, P], c=route_mem)
        B1 = sb("B1", [P, 2 * G, 2, NS], c=route_mem)
        e_lt = sb("e_lt", [1, NS, E], c=route_mem)
        e_f = sb("e_f", [1, NS], c=route_mem)
        route_mem.close()
        xg = sb("xg", [P, 2, D])
        gcol = [sb(f"gcol{r}", [P, 1], I32) for r in range(2)]
        scol = [sb(f"scol{r}", [P, 1], I32) for r in range(2)]
        xTe = sb("xTe", [P, 2, KF, P])
        sge = sb("sge", [P, 2, HID])
        ae = sb("ae", [P, 2, HID])
        aTe = sb("aTe", [P, 2, KH, P])
        ysc = sb("ysc", [P, 2, D])
        xn2_rows = nc.dram_tensor("xn2_rows", (G * P, D), F32).ap()
        row_sums = nc.dram_tensor("row_sums", (G * P + P, D), F32).ap()

        pssm = ExitStack()
        pA = ps("pA", [P, 4, P], pssm)
        pC = ps("pC", [P, 4, 4, P], pssm)
        pW = ps("pW", [P, 3, 512], pssm)
        pssm.close()
        p2 = ExitStack()
        pZ = ps("pZ", [P, 2, CH, BQ], p2)
        pX = ps("pX", [P, 2, 4, HH, T, AP_], p2)
        p2.close()
        tp = ps("tp", [P, 2, D])
        pR = ps("pR", [P, 512])
        pkv = ps("pkv", [P, 2 * D])
        pq = ps("pq", [P, 512])
        pg = ps("pg", [P, HID])
        pu = ps("pu", [P, HID])
        pa = ps("pa", [P, KH, P])
        py = ps("py", [P, 512])

        names = """ld_a ld_c0 ld_c1 ld_b ld_w ld_r ld_txt ld_sh ld_dt ld_bias id0 ident_ready consts
            ta_done tc_done tw_done tr_done exp_done b2_done wt_copied rwt_copied dve_ssm pool_ssm dc_ready
            q_pool_in q_dve w_in wr_ready wi_ready ssm_sum z_copied zt_done xa_copied xd_copied st1_done var1 sd1 rstd1_done
            xn1_ready t1_done xt1_ready proj_done kvq_ready ksq_ready n2_ready root_ready eps_added rn_ready kn_ready xs_copied nv_one var2_ready mean2_ready
            a1_done a2_done a3_done outer_ready u_ready tanh_done o_ready sq_ready sl_ready h1_ready x2_ready
            st2_done mv2_ready xn2_ready t2_done xt2_ready logit_done gs_done gu_done sg_ready m_done a_ready
            at_done at_ready y_done y_added logit_ready stored
            xn2_st0 xn2_st1 xn2_st2 ld_we rk_ready tables_ready route masks_ready counts_done exp2_done slots_ready onehot_ready place_ready slots_done tabs_ready
            sums_set gather_turn scatter_turn gcol_ready scol_ready gathered0 gathered1 ysc_ready scattered te_done xte_ready g_done sge_ready
            u_done ae_ready ate_done ate_ready ye_done""".split()
        s = {n: sem(n) for n in names}

        block = ctx.enter_context(nc.Block())

        xv = X[:, :, :].rearrange("p (c q) (a b) -> p c q a b", q=BT, b=BQ)

        AHEAD, LAST_LAG = 2 * BT, 8

        def run_experts(eng, step):
            for n in range(4):
                step(n, n % 2)
            with eng.Fori(2, NS // 2 - 1) as h:
                for r in range(2):
                    step(2 * h + r, r, h)
            for n in range(NS // 2 * 2 - 2, NS + 1):
                step(n, n % 2)

        def run(eng, step):
            lo, hi = 3 * BT, G - 2 * BT
            for g in range(lo):
                step(g, lambda lag, g=g: 0 <= g - lag < G)
            with eng.Fori(lo // BT, hi // BT) as t:
                for bt in range(BT):
                    step(t * BT + bt, lambda lag: True, bt, t)
            for g in range(hi, G + LAST_LAG):
                step(g, lambda lag, g=g: 0 <= g - lag < G)

        @block.sync
        def _(sp):
            sp.dma_start(inA[:], inv_A_real.rearrange("(q p) n -> p q n", p=P)).then_inc(s["ld_a"], 16)
            sp.dma_start(inI[:], A_imag.rearrange("(q p) n -> p q n", p=P)).then_inc(s["ld_a"], 16)
            for q in range(HH):
                sp.dma_start(dt[q * N:(q + 1) * N, :],
                             log_dt[q * P:(q + 1) * P].rearrange("(a h) -> a h", a=1).to_broadcast([N, P])
                             ).then_inc(s["ld_dt"], 16)
            for c in range(T):
                sp.dma_start(inC[:, c], x[c].rearrange("(q p) n r -> p q n r", p=P)
                             ).then_inc(s["ld_c0" if c < T // 2 else "ld_c1"], 16)
            sp.dma_start(xv_txt(X, BT), txt.rearrange("t p d -> p t d")).then_inc(s["ld_txt"], 16)
            sp.dma_start(sW13[:, 0], sw1[0].rearrange("(k p) n -> p k n", p=P)).then_inc(s["ld_sh"], 16)
            sp.dma_start(sW13[:, 1], sw3[0].rearrange("(k p) n -> p k n", p=P)).then_inc(s["ld_sh"], 16)
            sp.dma_start(sW2[:], sw2[0].rearrange("(k p) n -> p k n", p=P)).then_inc(s["ld_sh"], 16)

            def load_expert(e):
                for k, w in enumerate((w1, w3, w2)):
                    sp.dma_start(WE[:, e * EW + k * KF * HID:e * EW + (k + 1) * KF * HID].rearrange(
                        "p (k n) -> p k n", n=w.shape[2]), w[e].rearrange("(k p) n -> p k n", p=P)
                        ).then_inc(s["ld_we"], 16)

            def step(g, has, bt=None, t=None):
                b = g % BT if bt is None else bt
                if has(5):
                    i = g - 5
                    sp.wait_ge(s["xn2_ready"], i + 1)
                    rows = xn2_rows.rearrange("(g p) d -> p g d", p=P)[:, ix(i), :]
                    sp.dma_start(rows, xn2[:, (b - 5) % BT][:, None, :]).then_inc(s[f"xn2_st{(b - 5) % BT}"], 16)
                if t is None and g >= G - 2 * BT:
                    for e in range(E):
                        ready = min(4 * e + 4, G)
                        if max(ready, G - 2 * BT) == g:
                            sp.wait_ge(s["o_ready"], ready)
                            load_expert(e)

            run(sp, step)
            sp.wait_ge(s["y_added"], G)
            sp.dma_start(row_sums[0:G * P].rearrange("(g p) d -> p g d", p=P), X[:]).then_inc(s["sums_set"], 16)
            sp.wait_ge(s["scattered"], 16 * NS)
            sp.dma_start(out.rearrange("t r d -> (t r) d"), row_sums[0:G * P]).then_inc(s["stored"], 16)
            sp.wait_ge(s["stored"], 16)

        @block.gpsimd
        def _(pool):
            pool.memset(ident[:], 0.0).then_inc(s["id0"], 1)
            pool.wait_ge(s["id0"], 1)
            pool.affine_select(out=ident[:], in_=ident[:], compare_op=ALU.not_equal, fill=1.0, base=0,
                               pattern=[[-1, P]], channel_multiplier=1).then_inc(s["ident_ready"], 1)
            pool.memset(ones[:], 1.0).then_inc(s["tables_ready"], 1)
            pool.wait_ge(s["tables_ready"], 1)
            pool.affine_select(out=tri[:], in_=ones[:], compare_op=ALU.is_gt, fill=0.0, base=0,
                               pattern=[[1, P]], channel_multiplier=-1).then_inc(s["tables_ready"], 1)
            for table, pattern, base, per_row in ((iota, [[1, P]], 0, 0), (row1, [[P, G]], 1, 1),
                                                  (pad1, [[0, 1]], G * P + 1, 1), (steps, [[P, G]], 0, 0),
                                                  (rk, [[-1, E]], E, 0)):
                pool.iota(table[:], pattern=pattern, base=base, channel_multiplier=per_row,
                          allow_small_or_imprecise_dtypes=True).then_inc(s["tables_ready"], 1)
            n = 0
            for k, (A, top) in enumerate(doublings(Q, Pw, BQ, AP_)):
                m, w = top
                pool.wait_ge(s["q_pool_in"], k + 1)
                o = qt[:, 3, :, 0:w]
                pool.tensor_tensor(o, A[:, 1, :, 1:1 + w], A[:, 0, :, m:m + 1].to_broadcast([P, P, w]),
                                   ALU.mult).then_inc(s["pool_ssm"], 1)
                n += 1
                pool.wait_ge(s["pool_ssm"], n)
                pool.wait_ge(s["q_dve"], k + 1)
                pool.tensor_tensor(A[:, 1, :, m + 1:m + 1 + w], qt[:, 2, :, 0:w], o, ALU.add
                                   ).then_inc(s["pool_ssm"], 1)
                n += 1
            pool.wait_ge(s["dc_ready"], 2)
            for j in range(NCH):
                sl_ = slice(j * CH, (j + 1) * CH)
                d = Dc[:, 1, sl_, :, None].to_broadcast([P, CH, T, AP_])
                pp = Pw[:, 0, sl_, None, :].to_broadcast([P, CH, T, AP_])
                w4 = Wt[:, j % 2, 3].rearrange("p h (c a) -> p h c a", a=AP_)
                if j == 0:
                    pool.wait_ge(s["pool_ssm"], n)
                    pool.wait_ge(s["q_pool_in"], n // 2 + 1)
                pool.tensor_tensor(w4, d, pp, ALU.mult).then_inc(s["pool_ssm"], 1)
                n += 1
                pool.wait_ge(s["pool_ssm"], n)
                pool.wait_ge(s["w_in"], j + 1)
                if j >= 2:
                    pool.wait_ge(s["ssm_sum"], j - 1)
                pool.tensor_tensor(Wc[:, j % 2, 1], Wt[:, j % 2, 2], Wt[:, j % 2, 3], ALU.add
                                   ).then_inc(s["wi_ready"], 1)

            def step(g, has, bt=None, t=None):
                b = g % BT if bt is None else bt
                if has(-2):
                    kn(g + 2, (b + 2) % BT, (g + 2) // BT if t is None else t + (1 if b else 0))
                if has(0):
                    pool.wait_ge(s["tanh_done"], g + 1)
                    if gt(g, 0):
                        pool.wait_ge(s["sq_ready"], g)
                    q = KVQ[:, ix(g), 2].rearrange("p a (n j) -> p (a n) j", j=BLK)
                    pool.tensor_tensor(tq[:], S[:, b], q[:, :, None, :].to_broadcast([P, NB, BLK, BLK]),
                                       ALU.mult).then_inc(s["o_ready"], 1)
                if has(1):
                    c = (b - 1) % BT
                    pool.wait_ge(s["sl_ready"], g)
                    pool.tensor_tensor(sl[:, c], sl[:, c], Sq[:, c], ALU.mult).then_inc(s["h1_ready"], 1)
                    pool.wait_ge(s["h1_ready"], g)
                    if gt(g, BT):
                        pool.wait_ge(s["xs_copied"], g - BT)
                        pool.wait_ge(s["st2_done"], g - BT)
                    pool.tensor_tensor(xs[:, c], X[:, ix(g - 1)].rearrange("p a d -> p (a d)"), sl[:, c], ALU.add
                                       ).then_inc(s["x2_ready"], 1)

            def kn(i, b, ti):
                if b == 0:
                    pool.wait_ge(s["rn_ready"], ti + 1)
                k = KVQ[:, ix(i), 0].rearrange("p a (n j) -> p (a n) j", j=BLK)
                pool.tensor_tensor(k, k, rn[:, b * NB:(b + 1) * NB, None].to_broadcast([P, NB, BLK]), ALU.mult
                                   ).then_inc(s["kn_ready"], 1)

            kn(0, 0, 0)
            kn(1, 1, 0)
            run(pool, step)

            for j in range(0, 2 * G, CG):
                k, g, c = j // G, j % G, j // CG
                pool.wait_ge(s["onehot_ready"], c + 1)
                for w, by in enumerate((row1[:, g:g + CG, None], wt[:, k, g:g + CG, None])):
                    pool.tensor_tensor(B1[:, j:j + CG, w], eq[:, c % 2], by.to_broadcast([P, CG, NS]), ALU.mult
                                       ).then_inc(s["place_ready"], 1)

            def gather(n, r, h):
                pool.wait_ge(s["gcol_ready"], n + 1)
                if gt(n, 1):
                    pool.wait_ge(s["te_done"], n - 1)
                pool.sem_inc(s["gather_turn"], 1)
                pool.indirect_dma_start(out=xg[:, r], out_offset=None, in_=xn2_rows,
                                        in_offset=bass.IndirectOffsetOnAxis(ap=gcol[r][:], axis=0)
                                        ).then_inc(s[f"gathered{r}"], 16)

            for i in range(BT):
                pool.wait_ge(s[f"xn2_st{i}"], 16 * (G // BT))
            gather(0, 0, 0)
            gather(1, 1, 0)

            def expert(n, r, h=None):
                if not isinstance(n, int) or n + 2 < NS:
                    gather(n + 2, r, h)
                if 1 <= n <= NS if isinstance(n, int) else True:
                    pool.wait_ge(s["ysc_ready"], n)
                    pool.wait_ge(s["scol_ready"], n)
                    if gt(n, 1):
                        pool.wait_ge(s["scattered"], 16 * (n - 1))
                    else:
                        pool.wait_ge(s["sums_set"], 16)
                    pool.sem_inc(s["scatter_turn"], 1)
                    pool.indirect_dma_start(
                        out=row_sums, out_offset=bass.IndirectOffsetOnAxis(ap=scol[1 - r][:], axis=0),
                        in_=ysc[:, 1 - r], in_offset=None, compute_op=ALU.add).then_inc(s["scattered"], 16)

            run_experts(pool, expert)

        @block.scalar
        def _(act):
            act.dma_start(inB[:], B_ri.rearrange("(q p) n r -> p q n r", p=P)).then_inc(s["ld_b"], 16)
            for i, w in enumerate((W_k, W_v, W_q)):
                act.dma_start(wraw[:, i], w.rearrange("(k p) f -> p k f", p=P)).then_inc(s["ld_w"], 16)
            act.dma_start(rraw[:], router_w).then_inc(s["ld_r"], 16)
            act.dma_start(biasb[:], experts_bias.rearrange("(a e) -> a e", a=1).to_broadcast([P, E])
                          ).then_inc(s["ld_bias"], 16)
            act.wait_ge(s["ld_dt"], 16 * HH)
            act.activation(dt[:], dt[:], ACT.Exp).then_inc(s["exp_done"], 1)
            act.wait_ge(s["ta_done"], 1)
            act.activation(ea[:], pA[:, 0], ACT.Exp).then_inc(s["exp_done"], 1)
            act.mul(B2[:, 0], pA[:, 2], 2.0).then_inc(s["b2_done"], 1)
            act.mul(B2[:, 1], pA[:, 3], -2.0).then_inc(s["b2_done"], 1)
            act.mul(B2[:, 2], pA[:, 2], -2.0).then_inc(s["b2_done"], 1)
            act.wait_ge(s["tw_done"], 1)
            act.activation(wT[:].rearrange("p k (w o) -> p k w o", w=3), pW[:, :, :].rearrange(
                "p w (k o) -> p k w o", k=KF), ACT.Copy).then_inc(s["wt_copied"], 1)
            act.wait_ge(s["tr_done"], 1)
            act.activation(rwT[:], pA[:, 0, 0:KF * E].rearrange("p (k e) -> p k e", k=KF), ACT.Copy
                           ).then_inc(s["rwt_copied"], 1)
            for j in range(NCH):
                act.wait_ge(s["ssm_sum"], j + 1)
                act.activation(Z[:, :, j * CH:(j + 1) * CH].rearrange("p b h -> p h b"), pZ[:, j % 2], ACT.Copy
                               ).then_inc(s["z_copied"], 1)
            for j in range(BQ // 4):
                act.wait_ge(s["zt_done"], j + 1)
                act.activation(x_slot(xv, 0, j), pX[:, j % 2, :, 0], ACT.Copy).then_inc(s["xa_copied"], 1)
            act.wait_ge(s["var1"], 1)
            act.activation(rstd1[:], rstd1[:], ACT.Sqrt).then_inc(s["sd1"], 1)

            def front(i):
                act.wait_ge(s["t1_done"], i + 1)
                if gt(i, 0):
                    act.wait_ge(s["proj_done"], i)
                act.activation(xT1[:], tp[:, 0].rearrange("p (k n) -> p k n", k=KF), ACT.Copy
                               ).then_inc(s["xt1_ready"], 1)

            def front2(i):
                act.wait_ge(s["proj_done"], i + 1)
                kvq = KVQ[:, ix(i)].rearrange("p a w d -> p (a w) d")
                act.activation(kvq[:, 0:2], pkv[:].rearrange("p (w d) -> p w d", w=2), ACT.Copy
                               ).then_inc(s["kvq_ready"], 1)
                act.activation(kvq[:, 2], pq[:, 0:D], ACT.Copy).then_inc(s["kvq_ready"], 1)
                if gt(i, 0):
                    act.wait_ge(s["n2_ready"], i)
                act.activation(ksq[:].rearrange("p n j -> p (n j)"), pkv[:, 0:D], ACT.Square
                               ).then_inc(s["ksq_ready"], 1)

            def root(n):
                act.wait_ge(s["n2_ready"], min(n * BT + BT, G) if isinstance(n, int) else n * BT + BT)
                if gt(n, 0):
                    act.wait_ge(s["rn_ready"], n)
                act.activation(sd[:], nv[:], ACT.Sqrt).then_inc(s["root_ready"], 1)

            for i in range(AHEAD):
                front(i)
                front2(i)
                if i == BT - 1:
                    act.wait_ge(s["nv_one"], 1)
                    root(0)

            def step(g, has, bt=None, t=None):
                b = g % BT if bt is None else bt
                if has(-AHEAD):
                    front(g + AHEAD)
                if has(6):
                    i = g - 6
                    act.wait_ge(s["t2_done"], i + 1)
                    if gt(i, 0):
                        act.wait_ge(s["gu_done"], i)
                    act.activation(xT2[:], tp[:, 1].rearrange("p (k n) -> p k n", k=KF), ACT.Copy
                                   ).then_inc(s["xt2_ready"], 1)
                if b == 1 and any(map(has, (-2, 3, 4, 5))):
                    if has(3):
                        act.wait_ge(s["var2_ready"], g - 2)
                    root((g // BT if t is None else t) + 1)
                if has(3):
                    act.wait_ge(s["x2_ready"], g - 2)
                    act.activation(X[:, ix(g - 3)].rearrange("p a d -> p (a d)"), xs[:, (b - 3) % BT], ACT.Copy
                                   ).then_inc(s["xs_copied"], 1)
                if has(-AHEAD):
                    front2(g + AHEAD)
                if has(0):
                    act.wait_ge(s["u_ready"], g + 1)
                    act.activation(S[:, b], S[:, b], ACT.Tanh).then_inc(s["tanh_done"], 1)
                if has(1):
                    c = (b - 1) % BT
                    act.wait_ge(s["sq_ready"], g)
                    if gt(g, BT):
                        act.wait_ge(s["x2_ready"], g - BT)
                    act.activation(sl[:, c], Sq[:, c], ACT.Silu).then_inc(s["sl_ready"], 1)
                if has(6):
                    i = g - 6
                    act.wait_ge(s["gs_done"], i + 1)
                    if gt(i, 0):
                        act.wait_ge(s["m_done"], i)
                    act.activation(sg[:], pg[:], ACT.Silu).then_inc(s["sg_ready"], 1)
                if has(7):
                    i = g - 7
                    act.wait_ge(s["at_done"], i + 1)
                    if gt(i, 0):
                        act.wait_ge(s["y_done"], i)
                    act.activation(aT[:], pa[:], ACT.Copy).then_inc(s["at_ready"], 1)

            run(act, step)
            act.wait_ge(s["masks_ready"], 2)
            act.activation(wt[:, 1], den2[:], ACT.Exp).then_inc(s["exp2_done"], 1)

            def turned(n, r):
                act.wait_ge(s["te_done"], n + 1)
                if gt(n, 1):
                    act.wait_ge(s["u_done"], n - 1)
                act.activation(xTe[:, r], (pkv, pq)[r][:, 0:D].rearrange("p (k n) -> p k n", k=KF), ACT.Copy
                               ).then_inc(s["xte_ready"], 1)

            turned(0, 0)

            def expert(n, r, h=None):
                if not isinstance(n, int) or n < NS:
                    act.wait_ge(s["g_done"], n + 1)
                    if gt(n, 1):
                        act.wait_ge(s["ae_ready"], n - 1)
                    act.activation(sge[:, r], pg[:], ACT.Silu).then_inc(s["sge_ready"], 1)
                if 1 <= n <= NS if isinstance(n, int) else True:
                    act.wait_ge(s["ate_done"], n)
                    if gt(n, 2):
                        act.wait_ge(s["ye_done"], n - 2)
                    act.activation(aTe[:, 1 - r], pa[:], ACT.Copy).then_inc(s["ate_ready"], 1)
                if not isinstance(n, int) or n + 1 < NS:
                    turned(n + 1, 1 - r)

            run_experts(act, expert)

        @block.vector
        def _(dve):
            chain = [0]

            def link(ins):
                chain[0] += 1
                ins.then_inc(s["dve_ssm"], 1)
                dve.wait_ge(s["dve_ssm"], chain[0])

            dve.wait_ge(s["exp_done"], 2)
            dve.wait_ge(s["b2_done"], 3)
            link(dve.scalar_tensor_tensor(out=z[:, 0], in0=ea[:], scalar=-0.5, in1=dt[:], op0=ALU.mult, op1=ALU.mult))
            link(dve.scalar_tensor_tensor(out=z[:, 1], in0=pA[:, 1], scalar=0.5, in1=dt[:], op0=ALU.mult, op1=ALU.mult))
            link(dve.tensor_tensor(zz[:, 0:2], z[:], z[:], ALU.mult))
            link(dve.tensor_scalar(den[:, 0], z[:, 0], -1.0, 1.0, ALU.mult, ALU.add))
            link(dve.tensor_tensor(den[:, 1], den[:, 0], den[:, 0], ALU.mult))
            link(dve.tensor_tensor(den[:, 2], den[:, 1], zz[:, 1], ALU.add))
            link(dve.reciprocal(den[:, 3], den[:, 2]))
            link(dve.tensor_tensor(zz[:, 2], zz[:, 0], zz[:, 1], ALU.add))
            link(dve.tensor_scalar(zz[:, 0], zz[:, 2], -1.0, 1.0, ALU.mult, ALU.add))
            dve.memset(Q[:, 0, :, 0:1], 1.0)
            dve.memset(Q[:, 1, :, 0:1], 0.0)
            dve.memset(Pw[:, 0, :, 0:1], 1.0)
            dve.memset(Pw[:, 1, :, 0:1], 0.0)
            dve.tensor_tensor(Q[:, 0, :, 1], zz[:, 0], den[:, 3], ALU.mult).then_inc(s["dve_ssm"], 1)
            chain[0] += 1
            dve.scalar_tensor_tensor(out=Q[:, 1, :, 1], in0=z[:, 1], scalar=2.0, in1=den[:, 3], op0=ALU.mult,
                                     op1=ALU.mult).then_inc(s["q_pool_in"], 1)
            levels = list(doublings(Q, Pw, BQ, AP_))
            for k, (A, (m, w)) in enumerate(levels):
                if k == 0:
                    dve.wait_ge(s["q_pool_in"], 1)
                    dve.wait_ge(s["dve_ssm"], chain[0])
                br, bi = (A[:, r, :, m:m + 1].to_broadcast([P, P, w]) for r in range(2))
                ar, ai = (A[:, r, :, 1:1 + w] for r in range(2))
                if k > 0:
                    dve.wait_ge(s["pool_ssm"], 2 * k)
                    if A is not levels[k - 1][0]:
                        link(dve.tensor_copy(Pw[:, 0, :, 1], Q[:, 0, :, BQ]))
                        dve.tensor_scalar(Pw[:, 1, :, 1], Q[:, 1, :, BQ], -1.0, None, ALU.mult
                                          ).then_inc(s["q_pool_in"], 1)
                        dve.wait_ge(s["q_pool_in"], k + 1)
                dve.tensor_tensor(qt[:, 2, :, 0:w], ar, bi, ALU.mult).then_inc(s["q_dve"], 1)
                link(dve.tensor_tensor(qt[:, 0, :, 0:w], ar, br, ALU.mult))
                link(dve.tensor_tensor(qt[:, 1, :, 0:w], ai, bi, ALU.mult))
                dve.tensor_tensor(A[:, 0, :, m + 1:m + 1 + w], qt[:, 0, :, 0:w], qt[:, 1, :, 0:w], ALU.subtract
                                  ).then_inc(s["dve_ssm"], 1)
                chain[0] += 1
                dve.wait_ge(s["dve_ssm"], chain[0])
                if k + 1 < len(levels) and levels[k + 1][0] is A:
                    dve.wait_ge(s["pool_ssm"], 2 * k + 2)
                    dve.engine_nop().then_inc(s["q_pool_in"], 1)
                if k == 0:
                    pass
            dve.engine_nop().then_inc(s["q_pool_in"], 1)
            dve.wait_ge(s["tc_done"], 1)
            dve.wait_ge(s["b2_done"], 3)
            cr = pC[:].rearrange("p u v h -> p (u v) h").rearrange("p (c r) h -> p r h c", r=2)
            for o, (re, im) in enumerate(((0, 1), (1, 2))):
                d2 = [B2[:, i, :, None].to_broadcast([P, P, T]) for i in (re, im)]
                link(dve.tensor_tensor(Dc[:, o], cr[:, 0], d2[0], ALU.mult))
                link(dve.tensor_tensor(Dt[:, o], cr[:, 1], d2[1], ALU.mult))
                dve.tensor_tensor(Dc[:, o], Dc[:, o], Dt[:, o], ALU.add).then_inc(s["dc_ready"], 1)
            dve.wait_ge(s["dc_ready"], 2)
            dve.wait_ge(s["pool_ssm"], 2 * len(levels))
            nl = 2 * len(levels)
            for j in range(NCH):
                sl_ = slice(j * CH, (j + 1) * CH)
                d = [Dc[:, r, sl_, :, None].to_broadcast([P, CH, T, AP_]) for r in range(2)]
                pp = [Pw[:, r, sl_, None, :].to_broadcast([P, CH, T, AP_]) for r in range(2)]
                w4 = [Wt[:, j % 2, i].rearrange("p h (c a) -> p h c a", a=AP_) for i in range(4)]
                if j >= 2:
                    dve.wait_ge(s["wi_ready"], j - 1)
                dve.tensor_tensor(w4[2], d[0], pp[1], ALU.mult).then_inc(s["w_in"], 1)
                link(dve.tensor_tensor(w4[0], d[0], pp[0], ALU.mult))
                link(dve.tensor_tensor(w4[1], d[1], pp[1], ALU.mult))
                if j >= 2:
                    dve.wait_ge(s["ssm_sum"], j - 1)
                dve.tensor_tensor(Wc[:, j % 2, 0], Wt[:, j % 2, 0], Wt[:, j % 2, 1], ALU.subtract
                                  ).then_inc(s["wr_ready"], 1)
            dve.wait_ge(s["ld_txt"], 16)
            for g in range(BT - 1, G, BT):
                dve.bn_stats(st1[:, g], X[:, g]).then_inc(s["st1_done"], 1)
            for j in range(BQ // 4):
                dve.wait_ge(s["xa_copied"], j + 1)
                dve.tensor_copy(x_slot(xv, 1, j), pX[:, j % 2, :, 1]).then_inc(s["xd_copied"], 1)
            dve.wait_ge(s["xd_copied"], BQ // 4)
            for g in range(G):
                if g % BT < BT - 1:
                    dve.bn_stats(st1[:, g], X[:, g]).then_inc(s["st1_done"], 1)
            dve.wait_ge(s["st1_done"], G)
            for g in range(G):
                dve.bn_aggr(mv1[:, g], st1[:, g]).then_inc(s["st1_done"], 1)
            dve.wait_ge(s["st1_done"], 2 * G)
            dve.tensor_scalar(rstd1[:], mv1[:, :, 1], LN_EPS, None, ALU.add).then_inc(s["var1"], 1)
            dve.wait_ge(s["sd1"], 1)
            dve.reciprocal(rstd1[:], rstd1[:]).then_inc(s["rstd1_done"], 1)
            dve.wait_ge(s["rstd1_done"], 1)

            def rows(i, b):
                if gt(i, BT - 1):
                    dve.wait_ge(s["t1_done"], i - BT + 1)
                dve.tensor_scalar(xn1[:, b], X[:, ix(i)].rearrange("p a d -> p (a d)"),
                                  mv1[:, ix(i), 0:1].rearrange("p a b -> p (a b)"), rstd1[:, ix(i)],
                                  ALU.subtract, ALU.mult).then_inc(s["xn1_ready"], 1)

            def norm(i, b):
                dve.wait_ge(s["ksq_ready"], i + 1)
                dve.tensor_reduce(nv[:, b * NB:(b + 1) * NB], ksq[:], AX_X, ALU.add).then_inc(s["n2_ready"], 1)

            def roots(n):
                dve.wait_ge(s["root_ready"], n + 1)
                if gt(n, 0):
                    dve.wait_ge(s["kn_ready"], min(n * BT, G) if isinstance(n, int) else n * BT)
                dve.tensor_scalar(sd[:, 0:NN], sd[:, 0:NN], NORM_EPS, None, ALU.add).then_inc(s["eps_added"], 1)
                dve.wait_ge(s["eps_added"], n + 1)
                dve.reciprocal(rn[:], sd[:]).then_inc(s["rn_ready"], 1)

            dve.memset(nv[:], 1.0).then_inc(s["nv_one"], 1)
            dve.wait_ge(s["nv_one"], 1)
            dve.wait_ge(s["ld_bias"], 16)
            for i in range(BT):
                rows(i, i)
            for i in range(BT):
                norm(i, i)
                rows(i + BT, i)
            roots(0)
            for i in range(BT, AHEAD - 1):
                norm(i, i % BT)

            def read(i, b):
                k = KVQ[:, ix(i), 0].rearrange("p a (n j) -> p (a n) j", j=BLK)
                dve.wait_ge(s["kn_ready"], i + 1)
                dve.wait_ge(s["tanh_done"], i - BT + 1)
                dve.tensor_tensor(tmp[:, b], S[:, b], k[:, :, None, :].to_broadcast([P, NB, BLK, BLK]), ALU.mult
                                  ).then_inc(s["a1_done"], 1)

            def step(g, has, bt=None, t=None):
                b = g % BT if bt is None else bt
                ti = g // BT if t is None else t
                if has(-AHEAD):
                    rows(g + AHEAD, b)
                if has(3):
                    dve.wait_ge(s["st2_done"], g - 2)
                    if gt(g, 3):
                        dve.wait_ge(s["mean2_ready"], g - 3)
                        dve.wait_ge(s["var2_ready"], g - 3)
                if has(-1) and gt(g, BT - 2):
                    read(g + 1, (b + 1) % BT)
                if has(3):
                    dve.bn_aggr(ag[:], st2[:]).then_inc(s["mv2_ready"], 1)
                if has(7):
                    i = g - 7
                    dve.wait_ge(s["sg_ready"], i + 1)
                    dve.wait_ge(s["gu_done"], i + 1)
                    if gt(i, 0):
                        dve.wait_ge(s["at_done"], i)
                    dve.tensor_tensor(aa[:], sg[:], pu[:], ALU.mult).then_inc(s["m_done"], 1)
                if has(3):
                    c = (b - 3) % BT
                    dve.wait_ge(s["mv2_ready"], g - 2)
                    dve.tensor_copy(mean2[:, c:c + 1], ag[:, 0:1]).then_inc(s["mean2_ready"], 1)
                    dve.tensor_scalar(nv[:, NN + c:NN + c + 1], ag[:, 1:2], LN_EPS, None, ALU.add
                                      ).then_inc(s["var2_ready"], 1)
                if has(0) and gt(g, BT - 1):
                    kvq = KVQ[:, ix(g)].rearrange("p a w d -> p (a w) d")
                    k = kvq[:, 0].rearrange("p (n j) -> p n j", j=BLK)[:, :, None, :].to_broadcast([P, NB, BLK, BLK])
                    dve.wait_ge(s["a2_done"], g - BT + 1)
                    dve.tensor_tensor(dl[:], kvq[:, 1], pR[:, 0:D], ALU.subtract).then_inc(s["a3_done"], 1)
                if has(0) and gt(g, BT - 1):
                    dve.wait_ge(s["a3_done"], g - BT + 1)
                    dve.tensor_tensor(tmp[:, b], dl[:].rearrange("p (n i) -> p n i", i=BLK)[:, :, :, None]
                                      .to_broadcast([P, NB, BLK, BLK]), k, ALU.mult).then_inc(s["outer_ready"], 1)
                if has(7):
                    dve.wait_ge(s["logit_done"], g - 6)
                    if gt(g, 7):
                        dve.wait_ge(s["y_done"], g - 7)
                    dve.tensor_tensor(logits[:, ix(g - 7)].rearrange("p a e -> p (a e)"), py[:, D:D + E], biasb[:],
                                      ALU.add).then_inc(s["logit_ready"], 1)
                if has(8):
                    i = g - 8
                    xr = X[:, ix(i)].rearrange("p a d -> p (a d)")
                    dve.wait_ge(s["y_done"], i + 1)
                    dve.tensor_tensor(xr, xr, py[:, 0:D], ALU.add).then_inc(s["y_added"], 1)
                if has(-5):
                    if b == 1:
                        dve.wait_ge(s["root_ready"], ti + 2)
                    norm(g + 5, (b + 5) % BT)
                if b == 1 and any(map(has, (-2, 3, 4, 5))):
                    roots(ti + 1)
                if has(0) and gt(g, BT - 1):
                    dve.wait_ge(s["outer_ready"], g - BT + 1)
                    dve.wait_ge(s["o_ready"], g - 2)
                    dve.tensor_tensor(S[:, b], S[:, b], tmp[:, b], ALU.add).then_inc(s["u_ready"], 1)
                elif has(0):
                    kvq = KVQ[:, g]
                    k = kvq[:, 0].rearrange("p (n j) -> p n j", j=BLK)[:, :, None, :].to_broadcast([P, NB, BLK, BLK])
                    dve.wait_ge(s["kn_ready"], g + 1)
                    dve.tensor_tensor(S[:, b], kvq[:, 1].rearrange("p (n i) -> p n i", i=BLK)[:, :, :, None]
                                      .to_broadcast([P, NB, BLK, BLK]), k, ALU.mult).then_inc(s["u_ready"], 1)
                if has(1):
                    c = (b - 1) % BT
                    dve.wait_ge(s["o_ready"], g)
                    if gt(g, BT):
                        dve.wait_ge(s["h1_ready"], g - BT)
                    dve.tensor_reduce(Sq[:, c].rearrange("p (n i) -> p n i", i=BLK), tq[:], AX_X, ALU.add
                                      ).then_inc(s["sq_ready"], 1)
                if has(5):
                    i = g - 5
                    c = (b - 5) % BT
                    if b == 1:
                        dve.wait_ge(s["rn_ready"], ti + 2)
                    if gt(i, BT - 1):
                        dve.wait_ge(s["t2_done"], i - BT + 1)
                        dve.wait_ge(s[f"xn2_st{c}"], 16 * (ti - 2 + (1 if b == 2 else 0)))
                    dve.wait_ge(s["xs_copied"], i + 1)
                    dve.tensor_scalar(xn2[:, c], X[:, ix(i)].rearrange("p a d -> p (a d)"), mean2[:, c:c + 1],
                                      rn[:, NN + c:NN + c + 1], ALU.subtract, ALU.mult
                                      ).then_inc(s["xn2_ready"], 1)
                if has(2):
                    dve.wait_ge(s["x2_ready"], g - 1)
                    if has(3):
                        dve.wait_ge(s["mv2_ready"], g - 2)
                    dve.bn_stats(st2[:], xs[:, (b - 2) % BT]).then_inc(s["st2_done"], 1)

            run(dve, step)

            dve.wait_ge(s["tables_ready"], 7)
            dve.wait_ge(s["logit_ready"], G)
            full = [P, G, E]
            links = [0]

            def then(ins):
                links[0] += 1
                ins.then_inc(s["route"], 1)
                dve.wait_ge(s["route"], links[0])

            src = logits[:]
            for c in range(2):
                then(dve.tensor_reduce(top[:, c], src, AX_X, ALU.max))
                then(dve.tensor_tensor(va[:], src, top[:, c, :, None].to_broadcast(full), ALU.is_equal))
                then(dve.tensor_tensor(va[:], va[:], rk[:, None, :].to_broadcast(full), ALU.mult))
                then(dve.tensor_reduce(rb[:], va[:], AX_X, ALU.max))
                then(dve.tensor_tensor(M[:, c], va[:], rb[:, :, None].to_broadcast(full), ALU.is_equal))
                if c == 0:
                    then(dve.scalar_tensor_tensor(out=pos[:], in0=M[:, 0], scalar=-3.0e38, in1=logits[:],
                                                  op0=ALU.mult, op1=ALU.add))
                    src = pos[:]
            dve.tensor_tensor(Mc[:], M[:, 0], M[:, 1], ALU.add).then_inc(s["masks_ready"], 1)
            dve.tensor_tensor(den2[:], top[:, 1], top[:, 0], ALU.subtract).then_inc(s["masks_ready"], 1)
            tot = pu[:, 0:G * E].rearrange("p (g e) -> p g e", e=E)
            before = pg[:, 0:G * E].rearrange("p (g e) -> p g e", e=E)
            dve.wait_ge(s["counts_done"], 1)
            then(dve.tensor_copy(cnt[:, 0], tot))
            c, d = 0, 1
            while d < G:
                dve.tensor_copy(cnt[:, 1 - c, 0:d], cnt[:, c, 0:d])
                then(dve.tensor_tensor(cnt[:, 1 - c, d:], cnt[:, c, d:], cnt[:, c, 0:G - d], ALU.add))
                c, d = 1 - c, 2 * d
            dve.tensor_tensor(pos[:], cnt[:, c], tot, ALU.subtract).then_inc(s["route"], 1)
            links[0] += 1
            then(dve.tensor_tensor(over[:], cnt[:, c, G - 1, :, None].to_broadcast([P, E, G]),
                                   steps[:, None, :].to_broadcast([P, E, G]), ALU.is_gt))
            then(dve.tensor_reduce(ends[:, 2], over[:], AX_X, ALU.add))
            then(dve.tensor_copy(ends[:, 0], ends[:, 2]))
            c, d = 0, 1
            while d < E:
                dve.tensor_copy(ends[:, 1 - c, 0:d], ends[:, c, 0:d])
                then(dve.tensor_tensor(ends[:, 1 - c, d:], ends[:, c, d:], ends[:, c, 0:E - d], ALU.add))
                c, d = 1 - c, 2 * d
            ce = c
            then(dve.tensor_tensor(ends[:, 2], ends[:, c], ends[:, 2], ALU.subtract))
            then(dve.scalar_tensor_tensor(out=pos[:], in0=ends[:, 2, None, :].to_broadcast(full), scalar=float(P),
                                          in1=pos[:], op0=ALU.mult, op1=ALU.add))
            then(dve.tensor_tensor(pos[:], pos[:], before, ALU.add))
            then(dve.tensor_tensor(sp_[:], M[:], pos[:, None, :, :].to_broadcast([P, 2, G, E]), ALU.mult))
            then(dve.tensor_reduce(slot[:], sp_[:], AX_X, ALU.add))
            then(dve.tensor_copy(sloti[:, 0], slot[:]))
            dve.tensor_scalar(sloti[:, 1], sloti[:, 0], P.bit_length() - 1, None, ALU.arith_shift_right)
            then(dve.tensor_scalar(sloti[:, 2], sloti[:, 0], P - 1, None, ALU.bitwise_and))
            dve.tensor_copy(slotf[:], sloti[:, 1:3]).then_inc(s["slots_ready"], 1)
            dve.wait_ge(s["slots_ready"], 1)
            dve.wait_ge(s["exp2_done"], 1)
            then(dve.tensor_scalar(den2[:], wt[:, 1], 1.0, None, ALU.add))
            then(dve.reciprocal(wt[:, 0], den2[:]))
            then(dve.tensor_tensor(wt[:, 1], wt[:, 1], wt[:, 0], ALU.mult))
            for i in range(BT):
                dve.wait_ge(s[f"xn2_st{i}"], 16 * (G // BT))
            for j in range(0, 2 * G, CG):
                k, g = j // G, j % G
                c = j // CG
                if c >= 2:
                    dve.wait_ge(s["place_ready"], 2 * c - 2)
                dve.tensor_tensor(eq[:, c % 2], slotf[:, 0, k, g:g + CG, None].to_broadcast([P, CG, NS]),
                                  iota[:, None, 0:NS].to_broadcast([P, CG, NS]), ALU.is_equal
                                  ).then_inc(s["onehot_ready"], 1)
                dve.tensor_tensor(A1[:, j:j + CG], slotf[:, 1, k, g:g + CG, None].to_broadcast([P, CG, P]),
                                  iota[:, None, :].to_broadcast([P, CG, P]), ALU.is_equal
                                  ).then_inc(s["slots_ready"], 1)
            then(dve.tensor_tensor(e_lt[:], ends[0:1, ce, None, :].to_broadcast([1, NS, E]),
                                   iota[0:1, 0:NS, None].to_broadcast([1, NS, E]), ALU.is_le))
            then(dve.tensor_reduce(e_f[:], e_lt[:], AX_X, ALU.add))
            dve.tensor_scalar(etab[:], e_f[:], float(E - 1), None, ALU.min).then_inc(s["tabs_ready"], 1)
            pa_ = pa[:].rearrange("p k n -> p (k n)")
            dve.wait_ge(s["slots_done"], 1)
            dve.tensor_copy(wslot[:], pa_[:, NS:2 * NS]).then_inc(s["tabs_ready"], 1)
            dve.tensor_scalar(gidx[:], pa_[:, 0:NS], -1.0, 0.0, ALU.add, ALU.max).then_inc(s["tabs_ready"], 1)
            then(dve.tensor_scalar(sidx[:], pa_[:, 0:NS], 0.0, pad1[:], ALU.is_equal, ALU.mult))
            then(dve.tensor_tensor(sidx[:], sidx[:], pa_[:, 0:NS], ALU.add))
            dve.tensor_scalar(sidx[:], sidx[:], -1.0, None, ALU.add).then_inc(s["tabs_ready"], 1)
            dve.wait_ge(s["tabs_ready"], 4)

            for r in range(2):
                dve.tensor_copy(gcol[r][:], gidx[:, r:r + 1]).then_inc(s["gcol_ready"], 1)

            def expert(n, r, h=None):
                if not isinstance(n, int) or n + 2 < NS:
                    dve.wait_ge(s[f"gathered{r}"], 16 * (n // 2 + 1 if isinstance(n, int) else h + 1))
                    dve.wait_ge(s["tabs_ready"], 4)
                    dve.tensor_copy(gcol[r][:], gidx[:, ix(n + 2)]).then_inc(s["gcol_ready"], 1)
                if 1 <= n <= NS if isinstance(n, int) else True:
                    if gt(n, 2):
                        dve.wait_ge(s["scattered"], 16 * (n - 2))
                    dve.wait_ge(s["tabs_ready"], 4)
                    dve.tensor_copy(scol[1 - r][:], sidx[:, ix(n - 1)]).then_inc(s["scol_ready"], 1)
                if not isinstance(n, int) or n < NS:
                    if gt(n, 1):
                        dve.wait_ge(s["ate_done"], n - 1)
                    dve.wait_ge(s["sge_ready"], n + 1)
                    dve.wait_ge(s["u_done"], n + 1)
                    dve.tensor_tensor(ae[:, r], sge[:, r], pu[:], ALU.mult).then_inc(s["ae_ready"], 1)
                if 1 <= n <= NS if isinstance(n, int) else True:
                    dve.wait_ge(s["ye_done"], n)
                    dve.tensor_scalar(ysc[:, 1 - r], (py, pR)[r][:, 0:D], wslot[:, ix(n - 1)], None, ALU.mult
                                      ).then_inc(s["ysc_ready"], 1)

            run_experts(dve, expert)

        @block.tensor
        def _(pe):
            pe.wait_ge(s["ident_ready"], 1)
            pe.wait_ge(s["ld_a"], 32)
            pe.wait_ge(s["ld_b"], 16)
            bv = inB[:].rearrange("p q n r -> p r q n")
            for i, src in enumerate((inA[:], inI[:], bv[:, 0], bv[:, 1])):
                mm = pe.transpose(pA[:, i], src, ident[:])
            mm.then_inc(s["ta_done"], 1)
            for c in range(T):
                if c % (T // 2) == 0:
                    pe.wait_ge(s["ld_c0" if c == 0 else "ld_c1"], 16 * (T // 2))
                cv = inC[:, c].rearrange("p q n r -> p r q n")
                for r in range(2):
                    i = 2 * c + r
                    mm = pe.transpose(pC[:, i // 4, i % 4], cv[:, r], ident[:])
            mm.then_inc(s["tc_done"], 1)
            pe.wait_ge(s["ld_w"], 48)
            for w in range(3):
                for k in range(KF):
                    for o in range(KF):
                        mm = pe.transpose(pW[:, w, k * D + o * P:k * D + (o + 1) * P],
                                          wraw[:, w, o, k * P:(k + 1) * P], ident[:])
            mm.then_inc(s["tw_done"], 1)
            pe.wait_ge(s["ld_r"], 16)
            pe.wait_ge(s["q_pool_in"], 1)
            pe.wait_ge(s["b2_done"], 3)
            for k in range(KF):
                mm = pe.transpose(pA[:, 0, k * E:(k + 1) * E], rraw[:, k * P:(k + 1) * P], ident[0:E, 0:E])
            mm.then_inc(s["tr_done"], 1)

            pe.wait_ge(s["wt_copied"], 1)
            pe.wait_ge(s["rwt_copied"], 1)
            pe.wait_ge(s["dc_ready"], 2)
            for j in range(NCH):
                pe.wait_ge(s["wr_ready"], j + 1)
                pe.wait_ge(s["wi_ready"], j + 1)
                if j >= 2:
                    pe.wait_ge(s["z_copied"], j - 1)
                for h in range(CH):
                    for q in range(HH):
                        r0 = q * N
                        for r in range(2):
                            mm = pe.matmul(pZ[r0:r0 + CA, j % 2, h], Wc[r0:r0 + N, j % 2, r, h],
                                           Q[r0:r0 + N, r, j * CH + h, 0:BQ], start=(r == 0), stop=(r == 1))
                mm.then_inc(s["ssm_sum"], 1)
            pe.wait_ge(s["z_copied"], NCH)
            for j in range(BQ // 4):
                if j >= 2:
                    pe.wait_ge(s["xd_copied"], j - 1)
                for b in range(4):
                    mm = pe.transpose(pX[:, j % 2, b], Z[:, 4 * j + b], ident[:])
                mm.then_inc(s["zt_done"], 1)
            pe.wait_ge(s["xd_copied"], BQ // 4)

            def turn1(i, b):
                pe.wait_ge(s["xn1_ready"], i + 1)
                if gt(i, 0):
                    pe.wait_ge(s["xt1_ready"], i)
                if gt(i, 2 * AHEAD):
                    pe.wait_ge(s["xt2_ready"], i - 2 * AHEAD)
                for k in range(KF):
                    mm = pe.transpose(tp[:, 0, k * P:(k + 1) * P], xn1[:, b, k * P:(k + 1) * P], ident[:])
                mm.then_inc(s["t1_done"], 1)

            def project(i):
                pe.wait_ge(s["xt1_ready"], i + 1)
                if gt(i, 0):
                    pe.wait_ge(s["kvq_ready"], 2 * i)
                    pe.wait_ge(s["ksq_ready"], i)
                for k in range(KF):
                    pe.matmul(pkv[:], xT1[:, k], wT[:, k, 0:2 * D], start=(k == 0), stop=(k == KF - 1))
                    mm = pe.matmul(pq[:, 0:D], xT1[:, k], wT[:, k, 2 * D:3 * D], start=(k == 0), stop=(k == KF - 1))
                mm.then_inc(s["proj_done"], 1)

            for i in range(AHEAD):
                turn1(i, i % BT)
                project(i)
            pe.wait_ge(s["ld_sh"], 48)

            def read_sum(i, b):
                pe.wait_ge(s["a1_done"], i - BT + 1)
                if gt(i, BT):
                    pe.wait_ge(s["a3_done"], i - BT)
                for jj in range(BLK):
                    mm = pe.matmul(pR[:, 0:D], ident[:], tmp[:, b, :, :, jj], start=(jj == 0), stop=(jj == BLK - 1))
                mm.then_inc(s["a2_done"], 1)

            def step(g, has, bt=None, t=None):
                b = g % BT if bt is None else bt
                if has(-AHEAD):
                    turn1(g + AHEAD, b)
                if has(8):
                    i = g - 8
                    pe.wait_ge(s["at_ready"], i + 1)
                    if gt(i, 0):
                        pe.wait_ge(s["y_added"], i)
                    pe.wait_ge(s["logit_ready"], i + 1)
                    for k in range(KH):
                        mm = pe.matmul(py[:, 0:D], aT[:, k], sW2[:, k], start=(k == 0), stop=(k == KH - 1))
                    mm.then_inc(s["y_done"], 1)
                if has(-AHEAD):
                    project(g + AHEAD)
                if has(6):
                    i = g - 6
                    pe.wait_ge(s["xn2_ready"], i + 1)
                    pe.wait_ge(s["xt1_ready"], min(g + AHEAD + 1, G) if t is None else g + AHEAD + 1)
                    if gt(i, 0):
                        pe.wait_ge(s["xt2_ready"], i)
                    for k in range(KF):
                        mm = pe.transpose(tp[:, 1, k * P:(k + 1) * P], xn2[:, b, k * P:(k + 1) * P], ident[:])
                    mm.then_inc(s["t2_done"], 1)
                if has(-1) and gt(g, BT - 2):
                    read_sum(g + 1, (b + 1) % BT)
                if has(6):
                    i = g - 6
                    pe.wait_ge(s["xt2_ready"], i + 1)
                    if gt(i, 0):
                        pe.wait_ge(s["logit_ready"], i)
                        pe.wait_ge(s["sg_ready"], i)
                    if has(8):
                        pe.wait_ge(s["y_added"], i - 1)
                    for k in range(KF):
                        mm = pe.matmul(py[:, D:D + E], xT2[:, k], rwT[:, k], start=(k == 0), stop=(k == KF - 1))
                    mm.then_inc(s["logit_done"], 1)
                    for k in range(KF):
                        mm = pe.matmul(pg[:], xT2[:, k], sW13[:, 0, k], start=(k == 0), stop=(k == KF - 1))
                    mm.then_inc(s["gs_done"], 1)
                if has(7):
                    i = g - 7
                    pe.wait_ge(s["m_done"], i + 1)
                    if gt(i, 0):
                        pe.wait_ge(s["at_ready"], i)
                    for k in range(KH):
                        mm = pe.transpose(pa[:, k], aa[:, k * P:(k + 1) * P], ident[:])
                    mm.then_inc(s["at_done"], 1)
                if has(6):
                    for k in range(KF):
                        mm = pe.matmul(pu[:], xT2[:, k], sW13[:, 1, k], start=(k == 0), stop=(k == KF - 1))
                    mm.then_inc(s["gu_done"], 1)

            run(pe, step)
            pe.wait_ge(s["masks_ready"], 1)
            m = Mc[:].rearrange("p g e -> p (g e)")
            pe.matmul(pg[:, 0:G * E], tri[:], m, start=True, stop=True)
            pe.matmul(pu[:, 0:G * E], ones[:], m, start=True, stop=True).then_inc(s["counts_done"], 1)
            for j in range(2 * G):
                if j % CG == 0:
                    pe.wait_ge(s["slots_ready"], j // CG + 2)
                    pe.wait_ge(s["place_ready"], 2 * (j // CG) + 2)
                mm = pe.matmul(pa[:].rearrange("p k n -> p (k n)")[:, 0:2 * NS], A1[:, j],
                               B1[:, j].rearrange("p w n -> p (w n)"), start=(j == 0), stop=(j == 2 * G - 1))
            mm.then_inc(s["slots_done"], 1)
            pe.wait_ge(s["ld_we"], 16 * 3 * E)
            pe.wait_ge(s["tabs_ready"], 4)

            def turn(n, r, h):
                pe.wait_ge(s[f"gathered{r}"], 16 * (n // 2 + 1 if isinstance(n, int) else h + 1))
                if gt(n, 1):
                    pe.wait_ge(s["xte_ready"], n - 1)
                for k in range(KF):
                    mm = pe.transpose((pkv, pq)[r][:, k * P:(k + 1) * P], xg[:, r, k * P:(k + 1) * P], ident[:])
                mm.then_inc(s["te_done"], 1)

            turn(0, 0, 0)

            def weights(n):
                return nc.tensor.value_load(etab[0:1, ix(n)], min_val=0, max_val=E - 1) * EW

            def expert(n, r, h=None):
                now = not isinstance(n, int) or n < NS
                last = 1 <= n <= NS if isinstance(n, int) else True
                if now:
                    w = weights(n)
                    pe.wait_ge(s["xte_ready"], n + 1)
                    if gt(n, 0):
                        pe.wait_ge(s["sge_ready"], n)
                    for k in range(KF):
                        mm = pe.matmul(pg[:], xTe[:, r, k], WE[:, bass.ds(w + k * HID, HID)],
                                       start=(k == 0), stop=(k == KF - 1))
                    mm.then_inc(s["g_done"], 1)
                if last:
                    pe.wait_ge(s["ae_ready"], n)
                    if gt(n, 1):
                        pe.wait_ge(s["ate_ready"], n - 1)
                    for k in range(KH):
                        mm = pe.transpose(pa[:, k], ae[:, 1 - r, k * P:(k + 1) * P], ident[:])
                    mm.then_inc(s["ate_done"], 1)
                if not isinstance(n, int) or n + 1 < NS:
                    turn(n + 1, 1 - r, None if h is None else h + r)
                if now:
                    for k in range(KF):
                        mm = pe.matmul(pu[:], xTe[:, r, k], WE[:, bass.ds(w + (KF + k) * HID, HID)],
                                       start=(k == 0), stop=(k == KF - 1))
                    mm.then_inc(s["u_done"], 1)
                if last:
                    w = weights(n - 1)
                    pe.wait_ge(s["ate_ready"], n)
                    if gt(n, 2):
                        pe.wait_ge(s["ysc_ready"], n - 2)
                    for k in range(KH):
                        mm = pe.matmul((py, pR)[r][:, 0:D], aTe[:, 1 - r, k], WE[:, bass.ds(w + 2 * KF * HID + k * D, D)],
                                       start=(k == 0), stop=(k == KH - 1))
                    mm.then_inc(s["ye_done"], 1)

            run_experts(pe, expert)


def ix(i):
    return bass.ds(i, 1)


def gt(i, n):
    return not isinstance(i, int) or i > n


def doublings(Q, Pw, BQ, AP_):
    m = 1
    while m < BQ:
        yield Q, (m, m)
        m *= 2
    m = 1
    while m < AP_ - 1:
        yield Pw, (m, min(m, AP_ - 1 - m))
        m *= 2


def x_slot(xv, q, j):
    return xv[:, :, q, :, 4 * j:4 * j + 4].rearrange("p c a b -> p b c a")


def xv_txt(X, BT):
    return X[:, :, :].rearrange("p (t q) d -> p t q d", q=BT)[:, :, BT - 1, :]


_INS = ['x', 'txt', 'L0_tok_log_dt', 'L0_tok_inv_A_real', 'L0_tok_A_imag', 'L0_tok_B_ri', 'L0_attn_W_k',
        'L0_attn_W_v', 'L0_attn_W_q', 'L0_ffn_router_w', 'L0_ffn_experts_bias', 'L0_ffn_w1', 'L0_ffn_w3',
        'L0_ffn_w2', 'L0_ffn_sw1', 'L0_ffn_sw3', 'L0_ffn_sw2']
_OUTS = [((8, 384, 256), 'float32')]


def kernel(**inputs):
    import numpy as _np
    import concourse.bacc as _bacc
    from concourse import mybir as _mybir
    from concourse.bass_utils import run_bass_kernel_spmd as _run

    nc = _bacc.Bacc("TRN2", target_bir_lowering=False, num_devices=1)
    arrays, args = {}, []
    for name in _INS:
        a = _np.ascontiguousarray(inputs[name])
        arrays[f"in_{name}_dram"] = a
        args.append(nc.dram_tensor(f"in_{name}_dram", a.shape, _mybir.dt.from_np(a.dtype), kind="ExternalInput").ap())
    for i, (shape, dtype) in enumerate(_OUTS):
        dt = _mybir.dt.from_np(_np.dtype(dtype))
        args.append(nc.dram_tensor(f"out_{i}_dram", shape, dt, kind="ExternalOutput").ap())
    early_fusion_kernel(nc, *args)
    r = _run(nc, [arrays], core_ids=[0])
    return r.results[0]["out_0_dram"]
```

```python
from contextlib import ExitStack

import concourse.bass as bass
from concourse import mybir
from concourse.alu_op_type import AluOpType as ALU

F32 = mybir.dt.float32
F32R = mybir.dt.float32r
I32 = mybir.dt.int32
ACT = mybir.ActivationFunctionType
AX_X = mybir.AxisListType.X

P = 128
LN_EPS = 1e-5
NORM_EPS = 1e-6


def early_fusion_kernel(nc, x, txt, log_dt, inv_A_real, A_imag, B_ri, W_k, W_v, W_q,
                        router_w, experts_bias, w1, w3, w2, sw1, sw3, sw2, out):
    T, H, N, _ = x.shape
    TXT = txt.shape[1]
    D = txt.shape[2]
    HH = H // P
    BT = (H + TXT) // P
    G = T * BT
    BLK = 8
    NB = D // BLK
    E, HID = router_w.shape[0], w1.shape[2]
    KF = D // P
    KH = HID // P
    BQ = 32
    AP_ = D // BQ
    CA = T * AP_
    NS = 2 * G + E - 1
    LATE = G - 2 * BT
    CG = G // 2
    CH = 16
    NCH = P // CH
    NG = NCH // 2
    CW = P // NG

    with ExitStack() as ctx:
        def sb(name, shape, dt=F32, c=ctx):
            return c.enter_context(nc.sbuf_tensor(name, shape, dt))

        def ps(name, shape, c=ctx):
            return c.enter_context(nc.psum_tensor(name, shape, F32))

        def sem(name):
            return ctx.enter_context(nc.semaphore(name))

        rows_mem = ExitStack()
        wT = sb("wT", [P, KF, 3 * D], c=rows_mem)
        X = sb("X", [P, G, D], c=rows_mem)
        sg = sb("sg", [P, HID], c=rows_mem)
        rows_mem.close()
        W1h = sb("W1h", [P, E * KF * HID], F32R)
        ident = sb("ident", [P, P])
        rwT = sb("rwT", [P, KF, E])
        biasb = sb("biasb", [P, E])
        mv1 = sb("mv1", [P, G, 2])
        rstd1 = sb("rstd1", [P, G])
        st1 = sb("st1", [P, G, 6])
        sW13 = sb("sW13", [P, 2, KF, HID])
        sW2 = sb("sW2", [P, KH, D])
        logits = sb("logits", [P, G, E])
        aa = sb("aa", [P, BT, KH, P])
        late_mem = ExitStack()
        xTl = sb("xTl", [P, G - LATE, KF, P], c=late_mem)
        late_mem.close()
        xTr = sb("xTr", [P, 2, 2, KF, P], F32R)
        sb("xTl_rest", [P, G - LATE - 4, KF, P])
        tri = sb("tri", [P, P])
        ones = sb("ones", [P, P])
        iota = sb("iota", [P, P])
        row1 = sb("row1", [P, G])
        pad1 = sb("pad1", [P, 1])
        steps = sb("steps", [P, G])
        rk = sb("rk", [P, E])

        ssm = ExitStack()
        inA = sb("inA", [P, HH, N], c=ssm)
        inI = sb("inI", [P, HH, N], c=ssm)
        inB = sb("inB", [P, HH, N, 2], c=ssm)
        inC = sb("inC", [P, T, HH, N, 2], c=ssm)
        wraw = sb("wraw", [P, 3, KF, D], c=ssm)
        rraw = sb("rraw", [E, D], c=ssm)
        dt = sb("dt", [P, P], c=ssm)
        ea = sb("ea", [P, P], c=ssm)
        z = sb("z", [P, 2, P], c=ssm)
        zz = sb("zz", [P, 3, P], c=ssm)
        den = sb("den", [P, 4, P], c=ssm)
        B2 = sb("B2", [P, 4, P], c=ssm)
        Dc = sb("Dc", [P, 2, P, T], c=ssm)
        Dt = sb("Dt", [P, 2, P, T], c=ssm)
        Q = sb("Q", [P, 2, P, BQ + 1], c=ssm)
        Pw = sb("Pw", [P, 2, P, AP_], c=ssm)
        qt = sb("qt", [P, 4, P, BQ // 2], c=ssm)
        Wc = sb("Wc", [P, 2, 2, CH, CA], c=ssm)
        Wt = qt[:].rearrange("p i h w -> p (i h w)").rearrange("p (u i h w) -> p u i h w", u=2, i=4, h=CH)
        Z = sb("Z", [P, BQ, P], c=ssm)
        ssm.close()

        scan = ExitStack()
        KVQ = sb("KVQ", [P, G, 3, D], c=scan)
        S = sb("S", [P, BT, NB, BLK, BLK], c=scan)
        tmp = sb("tmp", [P, BT, NB, BLK, BLK], c=scan)
        tq = sb("tq", [P, NB, BLK, BLK], c=scan)
        xn1 = sb("xn1", [P, BT, D], c=scan)
        xT1 = sb("xT1", [P, KF, P], c=scan)
        ksq = sb("ksq", [P, NB, BLK], c=scan)
        NN = BT * NB
        nv = sb("nv", [P, NN + BT], c=scan)
        sd = sb("sd", [P, NN + BT], c=scan)
        rn = sb("rn", [P, NN + BT], c=scan)
        dl = sb("dl", [P, D], c=scan)
        Sq = sb("Sq", [P, BT, D], c=scan)
        sl = sb("sl", [P, BT, D], c=scan)
        st2 = sb("st2", [P, 6], c=scan)
        xs = sb("xs", [P, BT, D], c=scan)
        ag = sb("ag", [P, 2], c=scan)
        mean2 = sb("mean2", [P, BT], c=scan)
        xn2 = sb("xn2", [P, BT, D], c=scan)
        xT2 = xTl[:, G - LATE - 1]
        scan.close()

        EW = 2 * KF * HID
        we_mem = ExitStack()
        WE = sb("WE", [P, E * EW], c=we_mem)
        we_mem.close()
        WEl = sb("WEl", [P, E * EW], F32R)
        EV = KH * D
        raw_mem = ExitStack()
        W2 = sb("W2", [P, E * EV], c=raw_mem)
        raw_mem.close()
        W2l = sb("W2l", [P, E * EV], F32R)
        wslot = sb("wslot", [P, NS])
        gidx = sb("gidx", [P, NS])
        sidx = sb("sidx", [P, NS])
        etab = sb("etab", [1, NS], I32)
        route_mem = ExitStack()
        wt = sb("wt", [P, 2, G], c=route_mem)
        den2 = sb("den2", [P, G], c=route_mem)
        top = sb("top", [P, 2, G], c=route_mem)
        M = sb("M", [P, 2, G, E], c=route_mem)
        Mc = sb("Mc", [P, G, E], c=route_mem)
        va = sb("va", [P, G, E], c=route_mem)
        rb = sb("rb", [P, G], c=route_mem)
        cnt = sb("cnt", [P, 2, G, E], c=route_mem)
        pos = sb("pos", [P, G, E], c=route_mem)
        over = sb("over", [P, E, G], c=route_mem)
        ends = sb("ends", [P, 3, E], c=route_mem)
        slot_pos = sb("slot_pos", [P, 2, G, E], c=route_mem)
        slot = sb("slot", [P, 2, G], c=route_mem)
        sloti = sb("sloti", [P, 3, 2, G], I32, c=route_mem)
        slotf = sb("slotf", [P, 2, 2, G], c=route_mem)
        eq = sb("eq", [P, 2, CG, NS], c=route_mem)
        A1 = sb("A1", [P, 2 * G, P], c=route_mem)
        B1 = sb("B1", [P, 2, CG, 2, NS], c=route_mem)
        e_lt = sb("e_lt", [1, NS, E], c=route_mem)
        e_f = sb("e_f", [1, NS], c=route_mem)
        route_mem.close()
        xg = sb("xg", [P, 2, D])
        gcol = [sb(f"gcol{r}", [P, 1], I32) for r in range(2)]
        scol = [sb(f"scol{r}", [P, 1], I32) for r in range(2)]
        xTe = sb("xTe", [P, 2, KF, P])
        sge = sb("sge", [P, 2, HID])
        ae = aa[:, 0:2].rearrange("p r k n -> p r (k n)")
        aTe = sb("aTe", [P, 2, 2, KH, P], F32R)
        ysc = sb("ysc", [P, 2, D])
        W2h = sb("W2h", [P, E * EV], F32R)
        xn2_rows = nc.dram_tensor("xn2_rows", (G * P, D), F32).ap()
        row_sums = nc.dram_tensor("row_sums", (G * P + P, D), F32).ap()

        pssm = ExitStack()
        pA = ps("pA", [P, 4, P], pssm)
        pC = ps("pC", [P, 4, 4, P], pssm)
        pW = ps("pW", [P, 3, 512], pssm)
        pssm.close()
        p2 = ExitStack()
        pX = ps("pX", [P, 2, 4, HH, T, AP_], p2)
        ps("gap", [P, 3, 512], p2)
        pZ = ps("pZ", [P, 2, CH, BQ], p2)
        p2.close()
        tp = ps("tp", [P, 2, D])
        pR = ps("pR", [P, 512])
        pkv = ps("pkv", [P, 2 * D])
        pq = ps("pq", [P, 512])
        pg = ps("pg", [P, HID])
        pu = ps("pu", [P, HID])
        pa = ps("pa", [P, KH, P])
        py = ps("py", [P, 512])

        names = []
        names += """ld_a ld_c0 ld_c1 ld_b ld_w ld_r ld_txt ld_sh ld_dt ld_bias""".split()
        names += """id0 ident_ready ta_done tc_done tw_done tr_done exp_done b2_done wt_copied
                    rwt_copied dve_ssm pool_ssm dc_ready q_pool_in q_dve qi_ready w_in wr_ready wi_ready
                    ssm_sum z_copied zt_done xa_copied xd_copied st1_done var1 sd1 rstd1_done""".split()
        names += """xn1_ready t1_done xt1_ready proj_done kvq_ready ksq_ready n2_ready root_ready
                    eps_added rn_ready kn_ready xs_copied nv_one var2_ready mean2_ready a1_done a2_done
                    a3_done outer_ready u_ready tanh_done o_ready half_ready sq_ready sl_ready h1_ready
                    x2_ready st2_done mv2_ready xn2_ready t2_done xt2_ready logit_done gs_done gu_done
                    sg_ready m_done y_done y_added logit_ready""".split()
        names += """w1_high w1_low xtl_ready w2_high w2_low stored xn2_st0 xn2_st1 xn2_st2 ld_we ld_w2
                    tables_ready route masks_ready counts_done
                    exp2_done slots_ready onehot_ready place_ready onehot_used tabs_ready
                    sums_set0 sums_set1 sums_set2
                    gather_turn scatter_turn gcol_ready scol_ready gathered0 gathered1 ysc_ready
                    scattered te_done xte_ready g_done sge_ready u_done ae_ready ate_done ate_ready atl_ready
                    ye_done""".split()
        s = {n: sem(n) for n in names}

        block = ctx.enter_context(nc.Block())

        W1_GROUPS = [(e, 2) for e in range(0, E - 2, 2)] + [(E - 2, 1), (E - 1, 1)]

        def w1_high_of(e, m):
            return W1h[:, e * KF * HID:(e + m) * KF * HID].rearrange("p (e n) -> p e n", e=m)

        def w1_of(W, e, m):
            return W[:, e * EW:(e + m) * EW].rearrange("p (e n) -> p e n", e=m)[:, :, 0:KF * HID]

        xv = X[:, :, :].rearrange("p (c q) (a b) -> p c q a b", q=BT, b=BQ)

        AHEAD, LAST_LAG = 2 * BT, 7

        def run_experts(eng, step):
            for n in range(4):
                step(n, n % 2)
            with eng.Fori(2, NS // 2 - 1) as h:
                for r in range(2):
                    step(2 * h + r, r, h)
            for n in range(NS // 2 * 2 - 2, NS + 1):
                step(n, n % 2)

        def run(eng, step):
            lo, hi = 3 * BT, G - 2 * BT
            for g in range(lo):
                step(g, lambda lag, g=g: 0 <= g - lag < G)
            with eng.Fori(lo // BT, hi // BT) as t:
                for bt in range(BT):
                    step(t * BT + bt, lambda lag: True, bt, t)
            for g in range(hi, G + LAST_LAG):
                step(g, lambda lag, g=g: 0 <= g - lag < G)

        def late(i):
            return isinstance(i, int) and i >= LATE

        @block.sync
        def _(sp):
            sp.dma_start(inA[:], inv_A_real.rearrange("(q p) n -> p q n", p=P)).then_inc(s["ld_a"], 16)
            sp.dma_start(inI[:], A_imag.rearrange("(q p) n -> p q n", p=P)).then_inc(s["ld_a"], 16)
            for q in range(HH):
                sp.dma_start(dt[q * N:(q + 1) * N, :],
                             log_dt[q * P:(q + 1) * P].rearrange("(a h) -> a h", a=1).to_broadcast([N, P])
                             ).then_inc(s["ld_dt"], 16)
            for c in range(T):
                sp.dma_start(inC[:, c], x[c].rearrange("(q p) n r -> p q n r", p=P)
                             ).then_inc(s["ld_c0" if c < T // 2 else "ld_c1"], 16)
            sp.dma_start(xv_txt(X, BT), txt.rearrange("t p d -> p t d")).then_inc(s["ld_txt"], 16)
            sp.dma_start(sW13[:, 0], sw1[0].rearrange("(k p) n -> p k n", p=P)).then_inc(s["ld_sh"], 16)
            sp.dma_start(sW13[:, 1], sw3[0].rearrange("(k p) n -> p k n", p=P)).then_inc(s["ld_sh"], 16)
            sp.dma_start(sW2[:], sw2[0].rearrange("(k p) n -> p k n", p=P)).then_inc(s["ld_sh"], 16)

            def load_expert(e):
                for k, w in enumerate((w1, w3)):
                    sp.dma_start(WE[:, e * EW + k * KF * HID:e * EW + (k + 1) * KF * HID].rearrange(
                        "p (k n) -> p k n", n=HID), w[e].rearrange("(k p) n -> p k n", p=P)
                        ).then_inc(s["ld_we"], 16)

            left = [min(-(-(e + 1) * EW // (3 * D)), G) for e in range(E)]

            def step(g, has, bt=None, t=None):
                b = g % BT if bt is None else bt
                if has(5):
                    i = g - 5
                    sp.wait_ge(s["xn2_ready"], i + 1)
                    rows = xn2_rows.rearrange("(g p) d -> p g d", p=P)[:, ix(i), :]
                    sp.dma_start(rows, xn2[:, (b - 5) % BT][:, None, :]).then_inc(s[f"xn2_st{(b - 5) % BT}"], 16)
                if t is None and g >= G - 2 * BT:
                    for e in range(E):
                        if left[e] < G - 1 and max(left[e], G - 2 * BT) == g:
                            sp.wait_ge(s["o_ready"], left[e])
                            load_expert(e)

            run(sp, step)
            sp.wait_ge(s["o_ready"], G)
            for e in range(E):
                if left[e] >= G - 1:
                    load_expert(e)
            for e in range(E):
                sp.dma_start(W2[:, e * EV:(e + 1) * EV].rearrange("p (k n) -> p k n", n=D),
                             w2[e].rearrange("(k p) n -> p k n", p=P)).then_inc(s["ld_w2"], 16)
            for part, (lo, hi) in enumerate(((0, LATE), (LATE, G - 2), (G - 2, G))):
                sp.wait_ge(s["y_added"], hi)
                sp.dma_start(row_sums[lo * P:hi * P].rearrange("(g p) d -> p g d", p=P), X[:, lo:hi]
                             ).then_inc(s[f"sums_set{part}"], 16)
            sp.wait_ge(s["scattered"], 16 * NS)
            sp.dma_start(out.rearrange("t r d -> (t r) d"), row_sums[0:G * P]).then_inc(s["stored"], 16)
            sp.wait_ge(s["stored"], 16)

        @block.gpsimd
        def _(pool):
            pool.memset(ident[:], 0.0).then_inc(s["id0"], 1)
            pool.wait_ge(s["id0"], 1)
            pool.affine_select(out=ident[:], in_=ident[:], compare_op=ALU.not_equal, fill=1.0, base=0,
                               pattern=[[-1, P]], channel_multiplier=1).then_inc(s["ident_ready"], 1)
            pool.memset(ones[:], 1.0).then_inc(s["tables_ready"], 1)
            pool.wait_ge(s["tables_ready"], 1)
            pool.affine_select(out=tri[:], in_=ones[:], compare_op=ALU.is_gt, fill=0.0, base=0,
                               pattern=[[1, P]], channel_multiplier=-1).then_inc(s["tables_ready"], 1)
            for table, pattern, base, per_row in ((iota, [[1, P]], 0, 0), (row1, [[P, G]], 1, 1),
                                                  (pad1, [[0, 1]], G * P + 1, 1), (steps, [[P, G]], 0, 0),
                                                  (rk, [[-1, E]], E, 0)):
                pool.iota(table[:], pattern=pattern, base=base, channel_multiplier=per_row,
                          allow_small_or_imprecise_dtypes=True).then_inc(s["tables_ready"], 1)
            levels = list(doublings(Q, Pw, BQ, AP_))
            n = 0
            for gr in range(NG):
                cs = slice(gr * CW, (gr + 1) * CW)
                for k, (A, (m, w)) in enumerate(levels):
                    level = gr * len(levels) + k
                    pool.wait_ge(s["q_pool_in"], level + 1)
                    if k == 0 and gr > 0:
                        pool.wait_ge(s["wr_ready"], 2 * gr)
                        pool.wait_ge(s["wi_ready"], 2 * gr)
                    o = qt[:, 3, 0:CW, 0:w]
                    pool.tensor_tensor(o, A[:, 1, cs, 1:1 + w], A[:, 0, cs, m:m + 1].to_broadcast([P, CW, w]),
                                       ALU.mult).then_inc(s["pool_ssm"], 1)
                    n += 1
                    pool.wait_ge(s["pool_ssm"], n)
                    pool.wait_ge(s["q_dve"], level + 1)
                    pool.tensor_tensor(A[:, 1, cs, m + 1:m + 1 + w], qt[:, 2, 0:CW, 0:w], o, ALU.add
                                       ).then_inc(s["qi_ready"], 1)
                pool.wait_ge(s["dc_ready"], 2 * gr + 2)
                pool.wait_ge(s["q_pool_in"], (gr + 1) * len(levels) + 1)
                pool.wait_ge(s["qi_ready"], (gr + 1) * len(levels))
                for j in (2 * gr, 2 * gr + 1):
                    sl_ = slice(j * CH, (j + 1) * CH)
                    d = Dc[:, 1, sl_, :, None].to_broadcast([P, CH, T, AP_])
                    pp = Pw[:, 0, sl_, None, :].to_broadcast([P, CH, T, AP_])
                    w4 = Wt[:, j % 2, 3].rearrange("p h (c a) -> p h c a", a=AP_)
                    pool.tensor_tensor(w4, d, pp, ALU.mult).then_inc(s["pool_ssm"], 1)
                    n += 1
                    pool.wait_ge(s["pool_ssm"], n)
                    pool.wait_ge(s["w_in"], j + 1)
                    if j >= 2:
                        pool.wait_ge(s["ssm_sum"], j - 1)
                    pool.tensor_tensor(Wc[:, j % 2, 1], Wt[:, j % 2, 2], Wt[:, j % 2, 3], ALU.add
                                       ).then_inc(s["wi_ready"], 1)

            def step(g, has, bt=None, t=None):
                b = g % BT if bt is None else bt
                if has(-2):
                    kn(g + 2, (b + 2) % BT, (g + 2) // BT if t is None else t + (1 if b else 0))
                if has(0):
                    pool.wait_ge(s["tanh_done"], g + 1)
                    if gt(g, 0):
                        pool.wait_ge(s["sq_ready"], g)
                    q = KVQ[:, ix(g), 2].rearrange("p a (n j) -> p (a n) j", j=BLK)
                    pool.tensor_tensor(tq[:], S[:, b], q[:, :, None, :].to_broadcast([P, NB, BLK, BLK]),
                                       ALU.mult).then_inc(s["o_ready"], 1)
                    pool.wait_ge(s["o_ready"], g + 1)
                    pool.tensor_tensor(tq[:, :, :, 0:BLK // 2], tq[:, :, :, 0:BLK // 2], tq[:, :, :, BLK // 2:],
                                       ALU.add).then_inc(s["half_ready"], 1)
                if has(1):
                    c = (b - 1) % BT
                    pool.wait_ge(s["sl_ready"], g)
                    pool.tensor_tensor(sl[:, c], sl[:, c], Sq[:, c], ALU.mult).then_inc(s["h1_ready"], 1)
                    pool.wait_ge(s["h1_ready"], g)
                    if gt(g, BT):
                        pool.wait_ge(s["xs_copied"], g - BT)
                        pool.wait_ge(s["st2_done"], g - BT)
                    pool.tensor_tensor(xs[:, c], X[:, ix(g - 1)].rearrange("p a d -> p (a d)"), sl[:, c], ALU.add
                                       ).then_inc(s["x2_ready"], 1)

            def kn(i, b, ti):
                if b == 0:
                    pool.wait_ge(s["rn_ready"], ti + 1)
                k = KVQ[:, ix(i), 0].rearrange("p a (n j) -> p (a n) j", j=BLK)
                pool.tensor_tensor(k, k, rn[:, b * NB:(b + 1) * NB, None].to_broadcast([P, NB, BLK]), ALU.mult
                                   ).then_inc(s["kn_ready"], 1)

            kn(0, 0, 0)
            kn(1, 1, 0)
            run(pool, step)

            for j in range(0, 2 * G, CG):
                k, g, c = j // G, j % G, j // CG
                pool.wait_ge(s["onehot_ready"], c + 1)
                if c >= 2:
                    pool.wait_ge(s["onehot_used"], c - 1)
                for w, by in enumerate((row1[:, g:g + CG, None], wt[:, k, g:g + CG, None])):
                    pool.tensor_tensor(B1[:, c % 2, :, w], eq[:, c % 2], by.to_broadcast([P, CG, NS]), ALU.mult
                                       ).then_inc(s["place_ready"], 1)

            def gather(n, r):
                pool.wait_ge(s["gcol_ready"], n + 1)
                if gt(n, 1):
                    pool.wait_ge(s["te_done"], n - 1)
                pool.sem_inc(s["gather_turn"], 1)
                pool.indirect_dma_start(out=xg[:, r], out_offset=None, in_=xn2_rows,
                                        in_offset=bass.IndirectOffsetOnAxis(ap=gcol[r][:], axis=0)
                                        ).then_inc(s[f"gathered{r}"], 16)

            for i in range(BT):
                pool.wait_ge(s[f"xn2_st{i}"], 16 * (G // BT))
            gather(0, 0)
            gather(1, 1)
            for c in range(1, E // 2 - 1):
                q = slice(2 * c * EV, 2 * (c + 1) * EV)
                pool.wait_ge(s["w2_high"], c + 1)
                pool.tensor_tensor(W2l[:, q], W2[:, q], W2h[:, q], ALU.subtract).then_inc(s["w2_low"], 1)

            def expert(n, r, h=None):
                if not isinstance(n, int) or n + 2 < NS:
                    gather(n + 2, r)
                if 1 <= n <= NS if isinstance(n, int) else True:
                    pool.wait_ge(s["ysc_ready"], n)
                    pool.wait_ge(s["scol_ready"], n)
                    if gt(n, 1):
                        pool.wait_ge(s["scattered"], 16 * (n - 1))
                    else:
                        for part in range(3):
                            pool.wait_ge(s[f"sums_set{part}"], 16)
                    pool.sem_inc(s["scatter_turn"], 1)
                    pool.indirect_dma_start(
                        out=row_sums, out_offset=bass.IndirectOffsetOnAxis(ap=scol[1 - r][:], axis=0),
                        in_=ysc[:, 1 - r], in_offset=None, compute_op=ALU.add).then_inc(s["scattered"], 16)

            run_experts(pool, expert)

        @block.scalar
        def _(act):
            act.dma_start(inB[:], B_ri.rearrange("(q p) n r -> p q n r", p=P)).then_inc(s["ld_b"], 16)
            for i, w in enumerate((W_k, W_v, W_q)):
                act.dma_start(wraw[:, i], w.rearrange("(k p) f -> p k f", p=P)).then_inc(s["ld_w"], 16)
            act.dma_start(rraw[:], router_w).then_inc(s["ld_r"], 16)
            act.dma_start(biasb[:], experts_bias.rearrange("(a e) -> a e", a=1).to_broadcast([P, E])
                          ).then_inc(s["ld_bias"], 16)
            act.wait_ge(s["ld_dt"], 16 * HH)
            act.activation(dt[:], dt[:], ACT.Exp).then_inc(s["exp_done"], 1)
            act.wait_ge(s["ta_done"], 1)
            act.activation(ea[:], pA[:, 0], ACT.Exp).then_inc(s["exp_done"], 1)
            act.mul(B2[:, 0], pA[:, 2], 2.0).then_inc(s["b2_done"], 1)
            act.mul(B2[:, 1], pA[:, 3], -2.0).then_inc(s["b2_done"], 1)
            act.mul(B2[:, 2], pA[:, 2], -2.0).then_inc(s["b2_done"], 1)
            act.wait_ge(s["tw_done"], 1)
            act.activation(wT[:].rearrange("p k (w o) -> p k w o", w=3), pW[:, :, :].rearrange(
                "p w (k o) -> p k w o", k=KF), ACT.Copy).then_inc(s["wt_copied"], 1)
            act.wait_ge(s["tr_done"], 1)
            act.activation(rwT[:], pA[:, 0, 0:KF * E].rearrange("p (k e) -> p k e", k=KF), ACT.Copy
                           ).then_inc(s["rwt_copied"], 1)
            for j in range(NCH):
                act.wait_ge(s["ssm_sum"], j + 1)
                act.activation(Z[:, :, j * CH:(j + 1) * CH].rearrange("p b h -> p h b"), pZ[:, j % 2], ACT.Copy
                               ).then_inc(s["z_copied"], 1)
            for j in range(BQ // 4):
                act.wait_ge(s["zt_done"], j + 1)
                act.activation(x_slot(xv, 0, j), pX[:, j % 2, :, 0], ACT.Copy).then_inc(s["xa_copied"], 1)
            act.wait_ge(s["var1"], 1)
            act.activation(rstd1[:, 0:AHEAD], rstd1[:, 0:AHEAD], ACT.Sqrt).then_inc(s["sd1"], 1)

            def front(i):
                act.wait_ge(s["t1_done"], i + 1)
                if gt(i, 0):
                    act.wait_ge(s["proj_done"], i)
                act.activation(xT1[:], tp[:, 0].rearrange("p (k n) -> p k n", k=KF), ACT.Copy
                               ).then_inc(s["xt1_ready"], 1)

            def front2(i, kv=pkv, qq=pq):
                act.wait_ge(s["proj_done"], i + 1)
                kvq = KVQ[:, ix(i)].rearrange("p a w d -> p (a w) d")
                act.activation(kvq[:, 0:2], kv[:].rearrange("p (w d) -> p w d", w=2), ACT.Copy
                               ).then_inc(s["kvq_ready"], 1)
                act.activation(kvq[:, 2], qq[:, 0:D], ACT.Copy).then_inc(s["kvq_ready"], 1)
                if gt(i, 0):
                    act.wait_ge(s["n2_ready"], i)
                act.activation(ksq[:].rearrange("p n j -> p (n j)"), kv[:, 0:D], ACT.Square
                               ).then_inc(s["ksq_ready"], 1)

            def root(n):
                act.wait_ge(s["n2_ready"], min(n * BT + BT, G) if isinstance(n, int) else n * BT + BT)
                if gt(n, 0):
                    act.wait_ge(s["rn_ready"], n)
                act.activation(sd[:], nv[:], ACT.Sqrt).then_inc(s["root_ready"], 1)

            front(0)
            for i in range(AHEAD):
                if i + 1 < AHEAD:
                    front(i + 1)
                front2(i, *((pkv, pq), (pg, pu))[i % 2])
                if i == BT - 1:
                    act.wait_ge(s["nv_one"], 1)
                    root(0)
                    act.wait_ge(s["var1"], 2)
                    act.activation(rstd1[:, AHEAD:G], rstd1[:, AHEAD:G], ACT.Sqrt).then_inc(s["sd1"], 1)

            def state(g, b):
                act.wait_ge(s["u_ready"], g + 1)
                act.activation(S[:, b], S[:, b], ACT.Tanh).then_inc(s["tanh_done"], 1)

            def step(g, has, bt=None, t=None):
                b = g % BT if bt is None else bt
                if has(0) and not gt(g, BT - 1):
                    state(g, b)
                if has(-AHEAD):
                    front(g + AHEAD)
                if b == 1 and any(map(has, (-2, 3, 4, 5))):
                    if has(3):
                        act.wait_ge(s["var2_ready"], g - 2)
                    root((g // BT if t is None else t) + 1)
                if has(6):
                    i = g - 6
                    act.wait_ge(s["t2_done"], i + 1)
                    if gt(i, 0) and not late(i):
                        act.wait_ge(s["gu_done"], i)
                    act.activation(xT2 if not late(i) else xTl[:, i - LATE],
                                   tp[:, 1].rearrange("p (k n) -> p k n", k=KF), ACT.Copy
                                   ).then_inc(s["xt2_ready"], 1)
                if has(3):
                    act.wait_ge(s["x2_ready"], g - 2)
                    act.activation(X[:, ix(g - 3)].rearrange("p a d -> p (a d)"), xs[:, (b - 3) % BT], ACT.Copy
                                   ).then_inc(s["xs_copied"], 1)
                if has(-AHEAD):
                    front2(g + AHEAD)
                if has(0) and gt(g, BT - 1):
                    state(g, b)
                if has(1):
                    c = (b - 1) % BT
                    act.wait_ge(s["sq_ready"], g)
                    if gt(g, BT):
                        act.wait_ge(s["x2_ready"], g - BT)
                    act.activation(sl[:, c], Sq[:, c], ACT.Silu).then_inc(s["sl_ready"], 1)
                if has(6) and not late(g - 6):
                    i = g - 6
                    act.wait_ge(s["gs_done"], i + 1)
                    if gt(i, 0):
                        act.wait_ge(s["m_done"], i)
                    act.activation(sg[:], pg[:], ACT.Silu).then_inc(s["sg_ready"], 1)

            run(act, step)

            def w1_high(c):
                act.activation(w1_high_of(*W1_GROUPS[c]), w1_of(WE, *W1_GROUPS[c]), ACT.Copy
                               ).then_inc(s["w1_high"], 1)

            for i in range(LATE, G + 1):
                if i == LATE + 4:
                    act.wait_ge(s["ld_we"], 16 * 2 * E)
                    act.wait_ge(s["proj_done"], G)
                    act.wait_ge(s["sums_set0"], 16)
                    for c in range(len(W1_GROUPS) - 2):
                        w1_high(c)
                if i < G:
                    act.wait_ge(s["gs_done"], i + 1)
                    act.wait_ge(s["m_done"], i)
                    act.activation(sg[:], pg[:], ACT.Silu).then_inc(s["sg_ready"], 1)
                if i == LATE + 1:
                    act.wait_ge(s["masks_ready"], 2)
                    act.activation(wt[:, 1], den2[:], ACT.Exp).then_inc(s["exp2_done"], 1)

            act.wait_ge(s["ld_w2"], 16 * E)
            act.wait_ge(s["onehot_used"], 2 * G // CG)
            for c in range(E // 2):
                q = slice(2 * c * EV, 2 * (c + 1) * EV)
                act.activation(W2h[:, q], W2[:, q], ACT.Copy).then_inc(s["w2_high"], 1)
            act.wait_ge(s["sums_set1"], 16)
            w1_high(len(W1_GROUPS) - 2)

            def turned(n, r):
                turned_rows = (pkv, pq)[r][:, 0:D].rearrange("p (k n) -> p k n", k=KF)
                act.wait_ge(s["te_done"], n + 1)
                if gt(n, 1):
                    act.wait_ge(s["u_done"], n - 1)
                    act.wait_ge(s["xtl_ready"], n - 1)
                act.activation(xTr[:, r, 0], turned_rows, ACT.Copy).then_inc(s["xte_ready"], 1)
                act.activation(xTe[:, r], turned_rows, ACT.Copy).then_inc(s["xte_ready"], 1)

            turned(0, 0)
            act.wait_ge(s["sums_set2"], 16)
            w1_high(len(W1_GROUPS) - 1)

            def expert(n, r, h=None):
                if not isinstance(n, int) or n < NS:
                    act.wait_ge(s["g_done"], n + 1)
                    if gt(n, 1):
                        act.wait_ge(s["ae_ready"], n - 1)
                    act.activation(sge[:, r], pg[:], ACT.Silu).then_inc(s["sge_ready"], 1)
                if 1 <= n <= NS if isinstance(n, int) else True:
                    act.wait_ge(s["ate_done"], n)
                    if gt(n, 2):
                        act.wait_ge(s["ye_done"], n - 2)
                    act.activation(aTe[:, 1 - r, 0], pa[:], ACT.Copy).then_inc(s["ate_ready"], 1)
                if not isinstance(n, int) or n + 1 < NS:
                    turned(n + 1, 1 - r)

            run_experts(act, expert)

        @block.vector
        def _(dve):
            chain = [0]

            def link(ins):
                chain[0] += 1
                ins.then_inc(s["dve_ssm"], 1)
                dve.wait_ge(s["dve_ssm"], chain[0])

            dve.wait_ge(s["exp_done"], 2)
            dve.wait_ge(s["b2_done"], 3)
            link(dve.scalar_tensor_tensor(out=z[:, 0], in0=ea[:], scalar=-0.5, in1=dt[:], op0=ALU.mult, op1=ALU.mult))
            link(dve.scalar_tensor_tensor(out=z[:, 1], in0=pA[:, 1], scalar=0.5, in1=dt[:], op0=ALU.mult,
                                          op1=ALU.mult))
            link(dve.tensor_tensor(zz[:, 0:2], z[:], z[:], ALU.mult))
            link(dve.tensor_scalar(den[:, 0], z[:, 0], -1.0, 1.0, ALU.mult, ALU.add))
            link(dve.tensor_tensor(den[:, 1], den[:, 0], den[:, 0], ALU.mult))
            link(dve.tensor_tensor(den[:, 2], den[:, 1], zz[:, 1], ALU.add))
            link(dve.reciprocal(den[:, 3], den[:, 2]))
            link(dve.tensor_tensor(zz[:, 2], zz[:, 0], zz[:, 1], ALU.add))
            link(dve.tensor_scalar(zz[:, 0], zz[:, 2], -1.0, 1.0, ALU.mult, ALU.add))
            dve.memset(Q[:, 0, :, 0:1], 1.0)
            dve.memset(Q[:, 1, :, 0:1], 0.0)
            dve.memset(Pw[:, 0, :, 0:1], 1.0)
            dve.memset(Pw[:, 1, :, 0:1], 0.0)
            dve.tensor_tensor(Q[:, 0, :, 1], zz[:, 0], den[:, 3], ALU.mult).then_inc(s["dve_ssm"], 1)
            chain[0] += 1
            dve.scalar_tensor_tensor(out=Q[:, 1, :, 1], in0=z[:, 1], scalar=2.0, in1=den[:, 3], op0=ALU.mult,
                                     op1=ALU.mult).then_inc(s["q_pool_in"], 1)
            levels = list(doublings(Q, Pw, BQ, AP_))
            cr = pC[:].rearrange("p u v h -> p (u v) h").rearrange("p (c r) h -> p r h c", r=2)
            dve.wait_ge(s["q_pool_in"], 1)
            dve.wait_ge(s["dve_ssm"], chain[0])
            for gr in range(NG):
                cs = slice(gr * CW, (gr + 1) * CW)
                for k, (A, (m, w)) in enumerate(levels):
                    level = gr * len(levels) + k
                    if k == 0 and gr > 0:
                        dve.wait_ge(s["wi_ready"], 2 * gr)
                        dve.wait_ge(s["wr_ready"], 2 * gr)
                    if k > 0 and A is not levels[k - 1][0]:
                        dve.wait_ge(s["qi_ready"], level)
                        link(dve.tensor_copy(Pw[:, 0, cs, 1], Q[:, 0, cs, BQ]))
                        dve.tensor_scalar(Pw[:, 1, cs, 1], Q[:, 1, cs, BQ], -1.0, None, ALU.mult
                                          ).then_inc(s["q_pool_in"], 1)
                        dve.wait_ge(s["q_pool_in"], level + 1)
                    br, bi = (A[:, r, cs, m:m + 1].to_broadcast([P, CW, w]) for r in range(2))
                    ar, ai = (A[:, r, cs, 1:1 + w] for r in range(2))
                    dve.tensor_tensor(qt[:, 2, 0:CW, 0:w], ar, bi, ALU.mult).then_inc(s["q_dve"], 1)
                    dve.tensor_tensor(qt[:, 0, 0:CW, 0:w], ar, br, ALU.mult).then_inc(s["dve_ssm"], 1)
                    chain[0] += 1
                    link(dve.tensor_tensor(qt[:, 1, 0:CW, 0:w], ai, bi, ALU.mult))
                    link(dve.tensor_tensor(A[:, 0, cs, m + 1:m + 1 + w], qt[:, 0, 0:CW, 0:w], qt[:, 1, 0:CW, 0:w],
                                           ALU.subtract))
                    if k + 1 == len(levels) or levels[k + 1][0] is A:
                        dve.wait_ge(s["qi_ready"], level + 1)
                        dve.engine_nop().then_inc(s["q_pool_in"], 1)
                if gr == 0:
                    dve.wait_ge(s["tc_done"], 1)
                for o, (re, im) in enumerate(((0, 1), (1, 2))):
                    d2 = [B2[:, i, cs, None].to_broadcast([P, CW, T]) for i in (re, im)]
                    link(dve.tensor_tensor(Dc[:, o, cs], cr[:, 0, cs], d2[0], ALU.mult))
                    link(dve.tensor_tensor(Dt[:, o, cs], cr[:, 1, cs], d2[1], ALU.mult))
                    dve.tensor_tensor(Dc[:, o, cs], Dc[:, o, cs], Dt[:, o, cs], ALU.add).then_inc(s["dc_ready"], 1)
                dve.wait_ge(s["dc_ready"], 2 * gr + 2)
                for j in (2 * gr, 2 * gr + 1):
                    sl_ = slice(j * CH, (j + 1) * CH)
                    d = [Dc[:, r, sl_, :, None].to_broadcast([P, CH, T, AP_]) for r in range(2)]
                    pp = [Pw[:, r, sl_, None, :].to_broadcast([P, CH, T, AP_]) for r in range(2)]
                    w4 = [Wt[:, j % 2, i].rearrange("p h (c a) -> p h c a", a=AP_) for i in range(4)]
                    dve.tensor_tensor(w4[2], d[0], pp[1], ALU.mult).then_inc(s["w_in"], 1)
                    dve.tensor_tensor(w4[0], d[0], pp[0], ALU.mult).then_inc(s["dve_ssm"], 1)
                    chain[0] += 1
                    link(dve.tensor_tensor(w4[1], d[1], pp[1], ALU.mult))
                    if j >= 2:
                        dve.wait_ge(s["ssm_sum"], j - 1)
                    dve.tensor_tensor(Wc[:, j % 2, 0], Wt[:, j % 2, 0], Wt[:, j % 2, 1], ALU.subtract
                                      ).then_inc(s["wr_ready"], 1)
            dve.wait_ge(s["ld_txt"], 16)
            for g in range(BT - 1, G, BT):
                dve.bn_stats(st1[:, g], X[:, g]).then_inc(s["st1_done"], 1)
            for j in range(BQ // 4):
                dve.wait_ge(s["xa_copied"], j + 1)
                dve.tensor_copy(x_slot(xv, 1, j), pX[:, j % 2, :, 1]).then_inc(s["xd_copied"], 1)
            dve.wait_ge(s["xd_copied"], BQ // 4)
            counted = [G // BT]

            def statistics(tiles):
                for g in tiles:
                    if g % BT < BT - 1:
                        dve.bn_stats(st1[:, g], X[:, g]).then_inc(s["st1_done"], 1)
                        counted[0] += 1
                dve.wait_ge(s["st1_done"], counted[0])
                for g in tiles:
                    dve.bn_aggr(mv1[:, g], st1[:, g]).then_inc(s["st1_done"], 1)
                    counted[0] += 1
                dve.wait_ge(s["st1_done"], counted[0])
                dve.tensor_scalar(rstd1[:, tiles[0]:tiles[-1] + 1], mv1[:, tiles[0]:tiles[-1] + 1, 1], LN_EPS, None,
                                  ALU.add).then_inc(s["var1"], 1)

            statistics(range(AHEAD))
            dve.wait_ge(s["sd1"], 1)
            dve.reciprocal(rstd1[:, 0:AHEAD], rstd1[:, 0:AHEAD]).then_inc(s["rstd1_done"], 1)
            dve.wait_ge(s["rstd1_done"], 1)

            def rows(i, b):
                if gt(i, BT - 1):
                    dve.wait_ge(s["t1_done"], i - BT + 1)
                dve.tensor_scalar(xn1[:, b], X[:, ix(i)].rearrange("p a d -> p (a d)"),
                                  mv1[:, ix(i), 0:1].rearrange("p a b -> p (a b)"), rstd1[:, ix(i)],
                                  ALU.subtract, ALU.mult).then_inc(s["xn1_ready"], 1)

            def norm(i, b):
                dve.wait_ge(s["ksq_ready"], i + 1)
                dve.tensor_reduce(nv[:, b * NB:(b + 1) * NB], ksq[:], AX_X, ALU.add).then_inc(s["n2_ready"], 1)

            def roots(n):
                dve.wait_ge(s["root_ready"], n + 1)
                if gt(n, 0):
                    dve.wait_ge(s["kn_ready"], min(n * BT, G) if isinstance(n, int) else n * BT)
                dve.tensor_scalar(sd[:, 0:NN], sd[:, 0:NN], NORM_EPS, None, ALU.add).then_inc(s["eps_added"], 1)
                dve.wait_ge(s["eps_added"], n + 1)
                dve.reciprocal(rn[:], sd[:]).then_inc(s["rn_ready"], 1)

            dve.memset(nv[:], 1.0).then_inc(s["nv_one"], 1)
            dve.wait_ge(s["nv_one"], 1)
            dve.wait_ge(s["ld_bias"], 16)
            for i in range(BT):
                rows(i, i)
            statistics(range(AHEAD, G))
            for i in range(BT):
                norm(i, i)
                rows(i + BT, i)
            roots(0)
            dve.wait_ge(s["sd1"], 2)
            dve.reciprocal(rstd1[:, AHEAD:G], rstd1[:, AHEAD:G]).then_inc(s["rstd1_done"], 1)
            dve.wait_ge(s["rstd1_done"], 2)
            def read(i, b):
                k = KVQ[:, ix(i), 0].rearrange("p a (n j) -> p (a n) j", j=BLK)
                dve.wait_ge(s["kn_ready"], i + 1)
                dve.wait_ge(s["tanh_done"], i - BT + 1)
                dve.tensor_tensor(tmp[:, b], S[:, b], k[:, :, None, :].to_broadcast([P, NB, BLK, BLK]), ALU.mult
                                  ).then_inc(s["a1_done"], 1)

            def step(g, has, bt=None, t=None):
                b = g % BT if bt is None else bt
                ti = g // BT if t is None else t
                if has(0) and not gt(g, BT - 1):
                    kvq = KVQ[:, g]
                    k = kvq[:, 0].rearrange("p (n j) -> p n j", j=BLK)[:, :, None, :].to_broadcast([P, NB, BLK, BLK])
                    dve.wait_ge(s["kn_ready"], g + 1)
                    dve.tensor_tensor(S[:, b], kvq[:, 1].rearrange("p (n i) -> p n i", i=BLK)[:, :, :, None]
                                      .to_broadcast([P, NB, BLK, BLK]), k, ALU.mult).then_inc(s["u_ready"], 1)
                if t is None and g == 0:
                    for i in range(BT, AHEAD - 1):
                        norm(i, i % BT)
                if has(-AHEAD):
                    rows(g + AHEAD, b)
                if has(3):
                    dve.wait_ge(s["st2_done"], g - 2)
                    if gt(g, 3):
                        dve.wait_ge(s["mean2_ready"], g - 3)
                        dve.wait_ge(s["var2_ready"], g - 3)
                if has(-1) and gt(g, BT - 2):
                    read(g + 1, (b + 1) % BT)
                if has(3):
                    dve.bn_aggr(ag[:], st2[:]).then_inc(s["mv2_ready"], 1)
                if has(3):
                    c = (b - 3) % BT
                    dve.wait_ge(s["mv2_ready"], g - 2)
                    dve.tensor_copy(mean2[:, c:c + 1], ag[:, 0:1]).then_inc(s["mean2_ready"], 1)
                    dve.tensor_scalar(nv[:, NN + c:NN + c + 1], ag[:, 1:2], LN_EPS, None, ALU.add
                                      ).then_inc(s["var2_ready"], 1)
                if has(0) and gt(g, BT - 1):
                    kvq = KVQ[:, ix(g)].rearrange("p a w d -> p (a w) d")
                    k = kvq[:, 0].rearrange("p (n j) -> p n j", j=BLK)[:, :, None, :].to_broadcast([P, NB, BLK, BLK])
                    dve.wait_ge(s["a2_done"], g - BT + 1)
                    dve.tensor_tensor(dl[:], kvq[:, 1], pR[:, 0:D], ALU.subtract).then_inc(s["a3_done"], 1)
                if has(0) and gt(g, BT - 1):
                    dve.wait_ge(s["a3_done"], g - BT + 1)
                    dve.tensor_tensor(tmp[:, b], dl[:].rearrange("p (n i) -> p n i", i=BLK)[:, :, :, None]
                                      .to_broadcast([P, NB, BLK, BLK]), k, ALU.mult).then_inc(s["outer_ready"], 1)
                if has(7) and not late(g - 7):
                    i = g - 7
                    dve.wait_ge(s["sg_ready"], i + 1)
                    dve.wait_ge(s["gu_done"], i + 1)
                    if gt(i, BT - 1):
                        dve.wait_ge(s["y_done"], i - BT + 1)
                    dve.tensor_tensor(aa[:, (b - 7) % BT].rearrange("p k n -> p (k n)"), sg[:], pu[:], ALU.mult
                                      ).then_inc(s["m_done"], 1)
                if has(7):
                    dve.wait_ge(s["logit_done"], g - 6)
                    if gt(g, 7):
                        dve.wait_ge(s["y_done"], min(g - 7, LATE) if t is None else g - 7)
                    dve.tensor_tensor(logits[:, ix(g - 7)].rearrange("p a e -> p (a e)"), py[:, D:D + E], biasb[:],
                                      ALU.add).then_inc(s["logit_ready"], 1)
                if has(8) and not late(g - 8):
                    i = g - 8
                    xr = X[:, ix(i)].rearrange("p a d -> p (a d)")
                    dve.wait_ge(s["y_done"], i + 1)
                    dve.tensor_tensor(xr, xr, py[:, 0:D], ALU.add).then_inc(s["y_added"], 1)
                if has(-5):
                    if b == 1:
                        dve.wait_ge(s["root_ready"], ti + 2)
                    norm(g + 5, (b + 5) % BT)
                if b == 1 and any(map(has, (-2, 3, 4, 5))):
                    roots(ti + 1)
                if has(0) and gt(g, BT - 1):
                    dve.wait_ge(s["outer_ready"], g - BT + 1)
                    dve.wait_ge(s["o_ready"], g - 2)
                    dve.tensor_tensor(S[:, b], S[:, b], tmp[:, b], ALU.add).then_inc(s["u_ready"], 1)
                if has(1):
                    c = (b - 1) % BT
                    dve.wait_ge(s["half_ready"], g)
                    if gt(g, BT):
                        dve.wait_ge(s["h1_ready"], g - BT)
                    dve.tensor_reduce(Sq[:, c].rearrange("p (n i) -> p n i", i=BLK),
                                      tq[:, :, :, 0:BLK // 2], AX_X, ALU.add
                                      ).then_inc(s["sq_ready"], 1)
                if has(5):
                    i = g - 5
                    c = (b - 5) % BT
                    if b == 1:
                        dve.wait_ge(s["rn_ready"], ti + 2)
                    if gt(i, BT - 1):
                        dve.wait_ge(s["t2_done"], i - BT + 1)
                        dve.wait_ge(s[f"xn2_st{c}"], 16 * (ti - 2 + (1 if b == 2 else 0)))
                    dve.wait_ge(s["xs_copied"], i + 1)
                    dve.tensor_scalar(xn2[:, c], X[:, ix(i)].rearrange("p a d -> p (a d)"), mean2[:, c:c + 1],
                                      rn[:, NN + c:NN + c + 1], ALU.subtract, ALU.mult
                                      ).then_inc(s["xn2_ready"], 1)
                if has(2):
                    dve.wait_ge(s["x2_ready"], g - 1)
                    if has(3):
                        dve.wait_ge(s["mv2_ready"], g - 2)
                    dve.bn_stats(st2[:], xs[:, (b - 2) % BT]).then_inc(s["st2_done"], 1)

            run(dve, step)

            dve.wait_ge(s["tables_ready"], 7)
            dve.wait_ge(s["logit_ready"], G)
            full = [P, G, E]
            links = [0]

            def shared(i):
                if i < G:
                    dve.wait_ge(s["sg_ready"], i + 1)
                    dve.wait_ge(s["gu_done"], i + 1)
                    dve.wait_ge(s["y_done"], i - BT + 1)
                    dve.tensor_tensor(aa[:, i % BT].rearrange("p k n -> p (k n)"), sg[:], pu[:], ALU.mult
                                      ).then_inc(s["m_done"], 1)
                if i > LATE:
                    dve.wait_ge(s["y_done"], i)
                    dve.tensor_tensor(X[:, i - 1], X[:, i - 1], py[:, 0:D], ALU.add).then_inc(s["y_added"], 1)

            def then(ins):
                links[0] += 1
                ins.then_inc(s["route"], 1)
                dve.wait_ge(s["route"], links[0])

            src = logits[:]
            for c in range(2):
                then(dve.tensor_reduce(top[:, c], src, AX_X, ALU.max))
                then(dve.tensor_tensor(va[:], src, top[:, c, :, None].to_broadcast(full), ALU.is_equal))
                then(dve.tensor_tensor(va[:], va[:], rk[:, None, :].to_broadcast(full), ALU.mult))
                then(dve.tensor_reduce(rb[:], va[:], AX_X, ALU.max))
                then(dve.tensor_tensor(M[:, c], va[:], rb[:, :, None].to_broadcast(full), ALU.is_equal))
                if c == 0:
                    then(dve.scalar_tensor_tensor(out=pos[:], in0=M[:, 0], scalar=-3.0e38, in1=logits[:],
                                                  op0=ALU.mult, op1=ALU.add))
                    src = pos[:]
            dve.tensor_tensor(Mc[:], M[:, 0], M[:, 1], ALU.add).then_inc(s["masks_ready"], 1)
            dve.tensor_tensor(den2[:], top[:, 1], top[:, 0], ALU.subtract).then_inc(s["masks_ready"], 1)
            shared(LATE)
            tot = pq[:, 0:G * E].rearrange("p (g e) -> p g e", e=E)
            before = pkv[:, 0:G * E].rearrange("p (g e) -> p g e", e=E)
            dve.wait_ge(s["counts_done"], 1)
            then(dve.tensor_copy(cnt[:, 0], tot))
            c, d = 0, 1
            while d < G:
                dve.tensor_copy(cnt[:, 1 - c, 0:d], cnt[:, c, 0:d])
                then(dve.tensor_tensor(cnt[:, 1 - c, d:], cnt[:, c, d:], cnt[:, c, 0:G - d], ALU.add))
                c, d = 1 - c, 2 * d
            dve.tensor_tensor(pos[:], cnt[:, c], tot, ALU.subtract).then_inc(s["route"], 1)
            links[0] += 1
            shared(LATE + 1)
            then(dve.tensor_tensor(over[:], cnt[:, c, G - 1, :, None].to_broadcast([P, E, G]),
                                   steps[:, None, :].to_broadcast([P, E, G]), ALU.is_gt))
            then(dve.tensor_reduce(ends[:, 2], over[:], AX_X, ALU.add))
            then(dve.tensor_copy(ends[:, 0], ends[:, 2]))
            c, d = 0, 1
            while d < E:
                dve.tensor_copy(ends[:, 1 - c, 0:d], ends[:, c, 0:d])
                then(dve.tensor_tensor(ends[:, 1 - c, d:], ends[:, c, d:], ends[:, c, 0:E - d], ALU.add))
                c, d = 1 - c, 2 * d
            ce = c
            then(dve.tensor_tensor(ends[:, 2], ends[:, c], ends[:, 2], ALU.subtract))
            then(dve.scalar_tensor_tensor(out=pos[:], in0=ends[:, 2, None, :].to_broadcast(full), scalar=float(P),
                                          in1=pos[:], op0=ALU.mult, op1=ALU.add))
            then(dve.tensor_tensor(pos[:], pos[:], before, ALU.add))
            then(dve.tensor_tensor(slot_pos[:], M[:], pos[:, None, :, :].to_broadcast([P, 2, G, E]), ALU.mult))
            then(dve.tensor_reduce(slot[:], slot_pos[:], AX_X, ALU.add))
            then(dve.tensor_copy(sloti[:, 0], slot[:]))
            dve.tensor_scalar(sloti[:, 1], sloti[:, 0], P.bit_length() - 1, None, ALU.arith_shift_right)
            then(dve.tensor_scalar(sloti[:, 2], sloti[:, 0], P - 1, None, ALU.bitwise_and))
            dve.tensor_copy(slotf[:], sloti[:, 1:3]).then_inc(s["slots_ready"], 1)
            dve.wait_ge(s["slots_ready"], 1)
            shared(LATE + 2)
            dve.wait_ge(s["exp2_done"], 1)
            then(dve.tensor_scalar(den2[:], wt[:, 1], 1.0, None, ALU.add))
            then(dve.reciprocal(wt[:, 0], den2[:]))
            then(dve.tensor_tensor(wt[:, 1], wt[:, 1], wt[:, 0], ALU.mult))
            for i in range(BT):
                dve.wait_ge(s[f"xn2_st{i}"], 16 * (G // BT))
            for j in range(0, 2 * G, CG):
                k, g = j // G, j % G
                c = j // CG
                if c == 2:
                    shared(LATE + 3)
                if c >= 2:
                    dve.wait_ge(s["place_ready"], 2 * c - 2)
                dve.tensor_tensor(eq[:, c % 2], slotf[:, 0, k, g:g + CG, None].to_broadcast([P, CG, NS]),
                                  iota[:, None, 0:NS].to_broadcast([P, CG, NS]), ALU.is_equal
                                  ).then_inc(s["onehot_ready"], 1)
                dve.tensor_tensor(A1[:, j:j + CG], slotf[:, 1, k, g:g + CG, None].to_broadcast([P, CG, P]),
                                  iota[:, None, :].to_broadcast([P, CG, P]), ALU.is_equal
                                  ).then_inc(s["slots_ready"], 1)
            then(dve.tensor_tensor(e_lt[:], ends[0:1, ce, None, :].to_broadcast([1, NS, E]),
                                   iota[0:1, 0:NS, None].to_broadcast([1, NS, E]), ALU.is_le))
            then(dve.tensor_reduce(e_f[:], e_lt[:], AX_X, ALU.add))
            dve.tensor_scalar(etab[:], e_f[:], float(E - 1), None, ALU.min).then_inc(s["tabs_ready"], 1)
            shared(LATE + 4)

            def w1_low(c):
                dve.wait_ge(s["w1_high"], c + 1)
                dve.tensor_tensor(w1_of(WEl, *W1_GROUPS[c]), w1_of(WE, *W1_GROUPS[c]), w1_high_of(*W1_GROUPS[c]),
                                  ALU.subtract).then_inc(s["w1_low"], 1)

            w1_low(0)
            w1_low(1)
            pa_ = pR
            dve.wait_ge(s["onehot_used"], 2 * G // CG)
            dve.tensor_copy(wslot[:], pa_[:, NS:2 * NS]).then_inc(s["tabs_ready"], 1)
            dve.tensor_scalar(gidx[:], pa_[:, 0:NS], -1.0, 0.0, ALU.add, ALU.max).then_inc(s["tabs_ready"], 1)
            then(dve.tensor_scalar(sidx[:], pa_[:, 0:NS], 0.0, pad1[:], ALU.is_equal, ALU.mult))
            then(dve.tensor_tensor(sidx[:], sidx[:], pa_[:, 0:NS], ALU.add))
            dve.tensor_scalar(sidx[:], sidx[:], -1.0, None, ALU.add).then_inc(s["tabs_ready"], 1)
            dve.wait_ge(s["tabs_ready"], 4)

            for r in range(2):
                dve.tensor_copy(gcol[r][:], gidx[:, r:r + 1]).then_inc(s["gcol_ready"], 1)

            def rows_low(n, r):
                dve.wait_ge(s["xte_ready"], 2 * n + 2)
                dve.tensor_tensor(xTr[:, r, 1], xTe[:, r], xTr[:, r, 0], ALU.subtract).then_inc(s["xtl_ready"], 1)

            def low_part(c):
                q = slice(2 * c * EV, 2 * (c + 1) * EV)
                dve.wait_ge(s["w2_high"], c + 1)
                dve.tensor_tensor(W2l[:, q], W2[:, q], W2h[:, q], ALU.subtract).then_inc(s["w2_low"], 1)

            shared(LATE + 5)
            w1_low(2)
            shared(LATE + 6)
            low_part(0)
            w1_low(3)
            rows_low(0, 0)
            w1_low(4)
            low_part(E // 2 - 1)

            def expert(n, r, h=None):
                if not isinstance(n, int) or n + 2 < NS:
                    dve.wait_ge(s[f"gathered{r}"], 16 * (n // 2 + 1 if isinstance(n, int) else h + 1))
                    dve.wait_ge(s["tabs_ready"], 4)
                    dve.tensor_copy(gcol[r][:], gidx[:, ix(n + 2)]).then_inc(s["gcol_ready"], 1)
                if 1 <= n <= NS if isinstance(n, int) else True:
                    if gt(n, 2):
                        dve.wait_ge(s["scattered"], 16 * (n - 2))
                    dve.wait_ge(s["tabs_ready"], 4)
                    dve.tensor_copy(scol[1 - r][:], sidx[:, ix(n - 1)]).then_inc(s["scol_ready"], 1)
                if 1 <= n <= NS if isinstance(n, int) else True:
                    dve.wait_ge(s["ate_ready"], n)
                    if gt(n, 2):
                        dve.wait_ge(s["ye_done"], n - 2)
                    dve.tensor_tensor(aTe[:, 1 - r, 1], pa[:], aTe[:, 1 - r, 0], ALU.subtract
                                      ).then_inc(s["atl_ready"], 1)
                if not isinstance(n, int) or n + 1 < NS:
                    if gt(n, 1):
                        dve.wait_ge(s["g_done"], n)
                    rows_low(n + 1, 1 - r)
                if not isinstance(n, int) or n < NS:
                    if gt(n, 1):
                        dve.wait_ge(s["ate_done"], n - 1)
                    dve.wait_ge(s["sge_ready"], n + 1)
                    dve.wait_ge(s["u_done"], n + 1)
                    dve.tensor_tensor(ae[:, r], sge[:, r], pu[:], ALU.mult).then_inc(s["ae_ready"], 1)
                if 1 <= n <= NS if isinstance(n, int) else True:
                    dve.wait_ge(s["ye_done"], n)
                    dve.tensor_scalar(ysc[:, 1 - r], (py, pR)[r][:, 0:D], wslot[:, ix(n - 1)], None, ALU.mult
                                      ).then_inc(s["ysc_ready"], 1)

            run_experts(dve, expert)

        @block.tensor
        def _(pe):
            pe.wait_ge(s["ident_ready"], 1)
            pe.wait_ge(s["ld_a"], 32)
            pe.wait_ge(s["ld_b"], 16)
            bv = inB[:].rearrange("p q n r -> p r q n")
            for i, src in enumerate((inA[:], inI[:], bv[:, 0], bv[:, 1])):
                mm = pe.transpose(pA[:, i], src, ident[:])
            mm.then_inc(s["ta_done"], 1)
            for c in range(T):
                if c % (T // 2) == 0:
                    pe.wait_ge(s["ld_c0" if c == 0 else "ld_c1"], 16 * (T // 2))
                cv = inC[:, c].rearrange("p q n r -> p r q n")
                for r in range(2):
                    i = 2 * c + r
                    mm = pe.transpose(pC[:, i // 4, i % 4], cv[:, r], ident[:])
            mm.then_inc(s["tc_done"], 1)
            pe.wait_ge(s["ld_w"], 48)
            for w in range(3):
                for k in range(KF):
                    for o in range(KF):
                        mm = pe.transpose(pW[:, w, k * D + o * P:k * D + (o + 1) * P],
                                          wraw[:, w, o, k * P:(k + 1) * P], ident[:])
            mm.then_inc(s["tw_done"], 1)
            pe.wait_ge(s["ld_r"], 16)
            pe.wait_ge(s["q_pool_in"], 1)
            pe.wait_ge(s["b2_done"], 3)
            for k in range(KF):
                mm = pe.transpose(pA[:, 0, k * E:(k + 1) * E], rraw[:, k * P:(k + 1) * P], ident[0:E, 0:E])
            mm.then_inc(s["tr_done"], 1)

            pe.wait_ge(s["wt_copied"], 1)
            pe.wait_ge(s["rwt_copied"], 1)
            for j in range(NCH):
                pe.wait_ge(s["wr_ready"], j + 1)
                pe.wait_ge(s["wi_ready"], j + 1)
                if j >= 2:
                    pe.wait_ge(s["z_copied"], j - 1)
                for h in range(CH):
                    for q in range(HH):
                        r0 = q * N
                        for r in range(2):
                            mm = pe.matmul(pZ[r0:r0 + CA, j % 2, h], Wc[r0:r0 + N, j % 2, r, h],
                                           Q[r0:r0 + N, r, j * CH + h, 0:BQ], start=(r == 0), stop=(r == 1))
                mm.then_inc(s["ssm_sum"], 1)
            pe.wait_ge(s["z_copied"], NCH)
            pe.wait_ge(s["dc_ready"], 2 * NG)
            for j in range(BQ // 4):
                if j >= 2:
                    pe.wait_ge(s["xd_copied"], j - 1)
                for b in range(4):
                    mm = pe.transpose(pX[:, j % 2, b], Z[:, 4 * j + b], ident[:])
                mm.then_inc(s["zt_done"], 1)
            pe.wait_ge(s["xd_copied"], BQ // 4)

            def turn1(i, b):
                pe.wait_ge(s["xn1_ready"], i + 1)
                if gt(i, 0):
                    pe.wait_ge(s["xt1_ready"], i)
                if gt(i, 2 * AHEAD):
                    pe.wait_ge(s["xt2_ready"], i - 2 * AHEAD)
                for k in range(KF):
                    mm = pe.transpose(tp[:, 0, k * P:(k + 1) * P], xn1[:, b, k * P:(k + 1) * P], ident[:])
                mm.then_inc(s["t1_done"], 1)

            def project(i, kv=pkv, qq=pq, behind=0):
                pe.wait_ge(s["xt1_ready"], i + 1)
                if gt(i, behind):
                    pe.wait_ge(s["kvq_ready"], 2 * (i - behind))
                    pe.wait_ge(s["ksq_ready"], i - behind)
                for k in range(KF):
                    pe.matmul(kv[:], xT1[:, k], wT[:, k, 0:2 * D], start=(k == 0), stop=(k == KF - 1))
                    mm = pe.matmul(qq[:, 0:D], xT1[:, k], wT[:, k, 2 * D:3 * D], start=(k == 0), stop=(k == KF - 1))
                mm.then_inc(s["proj_done"], 1)

            for i in range(AHEAD):
                turn1(i, i % BT)
                project(i, *((pkv, pq), (pg, pu))[i % 2], 1)
            pe.wait_ge(s["ld_sh"], 48)

            def read_sum(i, b):
                pe.wait_ge(s["a1_done"], i - BT + 1)
                if gt(i, BT):
                    pe.wait_ge(s["a3_done"], i - BT)
                for jj in range(BLK):
                    mm = pe.matmul(pR[:, 0:D], ident[:], tmp[:, b, :, :, jj], start=(jj == 0), stop=(jj == BLK - 1))
                mm.then_inc(s["a2_done"], 1)

            def hidden(dst, w, xt):
                for c in range(KH):
                    for k in range(KF):
                        mm = pe.matmul(dst[:, c * P:(c + 1) * P], sW13[:, w, k, c * P:(c + 1) * P], xt[:, k],
                                       start=(k == 0), stop=(k == KF - 1))
                return mm

            def step(g, has, bt=None, t=None):
                b = g % BT if bt is None else bt
                if has(-AHEAD):
                    turn1(g + AHEAD, b)
                if has(8) and not late(g - 8):
                    i = g - 8
                    pe.wait_ge(s["m_done"], i + 1)
                    if gt(i, 0):
                        pe.wait_ge(s["y_added"], i)
                    pe.wait_ge(s["logit_ready"], i + 1)
                    for k in range(KH):
                        mm = pe.matmul(py[:, 0:D], aa[:, (b - 8) % BT, k], sW2[:, k],
                                       start=(k == 0), stop=(k == KH - 1))
                    mm.then_inc(s["y_done"], 1)
                if has(-AHEAD):
                    project(g + AHEAD)
                if has(6):
                    i = g - 6
                    pe.wait_ge(s["xn2_ready"], i + 1)
                    pe.wait_ge(s["xt1_ready"], min(g + AHEAD + 1, G) if t is None else g + AHEAD + 1)
                    if gt(i, 0):
                        pe.wait_ge(s["xt2_ready"], i)
                    for k in range(KF):
                        mm = pe.transpose(tp[:, 1, k * P:(k + 1) * P], xn2[:, b, k * P:(k + 1) * P], ident[:])
                    mm.then_inc(s["t2_done"], 1)
                if has(-1) and gt(g, BT - 2):
                    read_sum(g + 1, (b + 1) % BT)
                if has(6):
                    i = g - 6
                    pe.wait_ge(s["xt2_ready"], i + 1)
                    xt = xTl[:, i - LATE] if late(i) else xT2
                    if gt(i, 0):
                        pe.wait_ge(s["logit_ready"], i)
                        if not late(i):
                            pe.wait_ge(s["sg_ready"], i)
                    if has(8):
                        pe.wait_ge(s["y_added"], min(i - 1, LATE) if t is None else i - 1)
                    for k in range(KF):
                        mm = pe.matmul(py[:, D:D + E], xt[:, k], rwT[:, k], start=(k == 0), stop=(k == KF - 1))
                    mm.then_inc(s["logit_done"], 1)
                if has(6) and not late(g - 6):
                    hidden(pg, 0, xT2).then_inc(s["gs_done"], 1)
                if has(6) and not late(g - 6):
                    if gt(g, 6):
                        pe.wait_ge(s["m_done"], g - 6)
                    hidden(pu, 1, xT2).then_inc(s["gu_done"], 1)

            run(pe, step)
            def counts():
                pe.wait_ge(s["masks_ready"], 1)
                m = Mc[:].rearrange("p g e -> p (g e)")
                pe.matmul(pkv[:, 0:G * E], tri[:], m, start=True, stop=True)
                pe.matmul(pq[:, 0:G * E], ones[:], m, start=True, stop=True).then_inc(s["counts_done"], 1)

            def fill_slots(c):
                pe.wait_ge(s["slots_ready"], c + 2)
                pe.wait_ge(s["place_ready"], 2 * c + 2)
                for j in range(CG):
                    i = c * CG + j
                    mm = pe.matmul(pR[:, 0:2 * NS], A1[:, i], B1[:, c % 2, j].rearrange("p w n -> p (w n)"),
                                   start=(i == 0), stop=(i == 2 * G - 1))
                mm.then_inc(s["onehot_used"], 1)

            for i in range(LATE, G + 1):
                if i < G:
                    pe.wait_ge(s["sg_ready"], i)
                    hidden(pg, 0, xTl[:, i - LATE]).then_inc(s["gs_done"], 1)
                if i == LATE + 1:
                    counts()
                if i < G:
                    pe.wait_ge(s["m_done"], i)
                    hidden(pu, 1, xTl[:, i - LATE]).then_inc(s["gu_done"], 1)
                if i > LATE:
                    pe.wait_ge(s["m_done"], i)
                    pe.wait_ge(s["y_added"], i - 1)
                    pe.wait_ge(s["logit_ready"], G)
                    for k in range(KH):
                        mm = pe.matmul(py[:, 0:D], aa[:, (i - 1) % BT, k], sW2[:, k],
                                       start=(k == 0), stop=(k == KH - 1))
                    mm.then_inc(s["y_done"], 1)
                if i in (LATE + 3, LATE + 4):
                    fill_slots(2 * (i - LATE - 3))
                    fill_slots(2 * (i - LATE - 3) + 1)
            pe.wait_ge(s["tabs_ready"], 4)

            def turn(n, r, h):
                pe.wait_ge(s[f"gathered{r}"], 16 * (n // 2 + 1 if isinstance(n, int) else h + 1))
                if gt(n, 1):
                    pe.wait_ge(s["xte_ready"], 2 * n - 2)
                for k in range(KF):
                    mm = pe.transpose((pkv, pq)[r][:, k * P:(k + 1) * P], xg[:, r, k * P:(k + 1) * P], ident[:])
                mm.then_inc(s["te_done"], 1)

            turn(0, 0, 0)

            expert_reg = [pe.alloc_register(f"expert_reg{r}") for r in range(2)]

            def load_expert(n, r):
                pe.reg_load(expert_reg[r], etab[0:1, ix(n)])

            def expert_of(r):
                return pe.snap(expert_reg[r], min_val=0, max_val=E - 1)

            load_expert(0, 0)

            def expert(n, r, h=None):
                now = not isinstance(n, int) or n < NS
                last = 1 <= n <= NS if isinstance(n, int) else True
                if now:
                    chosen = expert_of(r)
                    w, w_h = chosen * EW, chosen * (KF * HID)
                    pe.wait_ge(s["xtl_ready"], n + 1)
                    if n == 0 if isinstance(n, int) else False:
                        pe.wait_ge(s["w1_low"], len(W1_GROUPS))
                    if gt(n, 0):
                        pe.wait_ge(s["sge_ready"], n)
                    for k in range(KF):
                        high, low = W1h[:, bass.ds(w_h + k * HID, HID)], WEl[:, bass.ds(w + k * HID, HID)]
                        for i, (x_part, w_part) in enumerate(((0, high), (1, high), (0, low))):
                            mm = pe.matmul(pg[:], xTr[:, r, x_part, k], w_part,
                                           start=(k == 0 and i == 0), stop=(k == KF - 1 and i == 2))
                    mm.then_inc(s["g_done"], 1)
                if last:
                    pe.wait_ge(s["ae_ready"], n)
                    if gt(n, 1):
                        pe.wait_ge(s["atl_ready"], n - 1)
                    for k in range(KH):
                        mm = pe.transpose(pa[:, k], ae[:, 1 - r, k * P:(k + 1) * P], ident[:])
                    mm.then_inc(s["ate_done"], 1)
                if not isinstance(n, int) or n + 1 < NS:
                    turn(n + 1, 1 - r, None if h is None else h + r)
                if now:
                    for k in range(KF):
                        mm = pe.matmul(pu[:], xTe[:, r, k], WE[:, bass.ds(w + (KF + k) * HID, HID)],
                                       start=(k == 0), stop=(k == KF - 1))
                    mm.then_inc(s["u_done"], 1)
                if last:
                    w = expert_of(1 - r) * EV
                if not isinstance(n, int) or n + 1 < NS:
                    load_expert(n + 1, 1 - r)
                if last:
                    pe.wait_ge(s["atl_ready"], n)
                    if n == 1 if isinstance(n, int) else False:
                        pe.wait_ge(s["w2_low"], E // 2)
                    if gt(n, 2):
                        pe.wait_ge(s["ysc_ready"], n - 2)
                    for k in range(KH):
                        v = bass.ds(w + k * D, D)
                        for i, (x_part, w_part) in enumerate(((0, W2h), (0, W2l), (1, W2h))):
                            mm = pe.matmul((py, pR)[r][:, 0:D], aTe[:, 1 - r, x_part, k], w_part[:, v],
                                           start=(k == 0 and i == 0), stop=(k == KH - 1 and i == 2))
                    mm.then_inc(s["ye_done"], 1)

            run_experts(pe, expert)


def ix(i):
    return bass.ds(i, 1)


def gt(i, n):
    return not isinstance(i, int) or i > n


def doublings(Q, Pw, BQ, AP_):
    m = 1
    while m < BQ:
        yield Q, (m, m)
        m *= 2
    m = 1
    while m < AP_ - 1:
        yield Pw, (m, min(m, AP_ - 1 - m))
        m *= 2


def x_slot(xv, q, j):
    return xv[:, :, q, :, 4 * j:4 * j + 4].rearrange("p c a b -> p b c a")


def xv_txt(X, BT):
    return X[:, :, :].rearrange("p (t q) d -> p t q d", q=BT)[:, :, BT - 1, :]


_INS = ['x', 'txt', 'L0_tok_log_dt', 'L0_tok_inv_A_real', 'L0_tok_A_imag', 'L0_tok_B_ri', 'L0_attn_W_k',
        'L0_attn_W_v', 'L0_attn_W_q', 'L0_ffn_router_w', 'L0_ffn_experts_bias', 'L0_ffn_w1', 'L0_ffn_w3',
        'L0_ffn_w2', 'L0_ffn_sw1', 'L0_ffn_sw3', 'L0_ffn_sw2']
_OUTS = [((8, 384, 256), 'float32')]


def kernel(**inputs):
    import numpy as _np
    import concourse.bacc as _bacc
    from concourse import mybir as _mybir
    from concourse.bass_utils import run_bass_kernel_spmd as _run

    nc = _bacc.Bacc("TRN2", target_bir_lowering=False, num_devices=1)
    arrays, args = {}, []
    for name in _INS:
        a = _np.ascontiguousarray(inputs[name])
        arrays[f"in_{name}_dram"] = a
        args.append(nc.dram_tensor(f"in_{name}_dram", a.shape, _mybir.dt.from_np(a.dtype), kind="ExternalInput").ap())
    for i, (shape, dtype) in enumerate(_OUTS):
        dt = _mybir.dt.from_np(_np.dtype(dtype))
        args.append(nc.dram_tensor(f"out_{i}_dram", shape, dt, kind="ExternalOutput").ap())
    early_fusion_kernel(nc, *args)
    r = _run(nc, [arrays], core_ids=[0])
    return r.results[0]["out_0_dram"]
```
